# Optimizing a Trainium2 kernel written in Bass

```python
import numpy as np
import jax
import jax.numpy as jnp

def _softmax(x, axis=-1):
    return jax.nn.softmax(x, axis=axis)

def _gelu(x):
    return jax.nn.gelu(x, approximate=True)

def _silu(x):
    return jax.nn.silu(x)

def _sigmoid(x):
    return jax.nn.sigmoid(x)

def _layernorm(x, axis=-1, eps=1e-05):
    m = jnp.mean(x, axis=axis, keepdims=True)
    v = jnp.var(x, axis=axis, keepdims=True)
    return (x - m) / jnp.sqrt(v + eps)

def _scatter_add(tgt, idx, src, axis=0):
    return tgt.at[idx].add(src)

def _segment_sum(src, seg, n):
    return jax.ops.segment_sum(src, seg, n)
kernel_name = 'mk_xattn_ffn_d2_seqx_r8_d02bc0'

def setup_inputs(seed: int=0):
    np.random.seed(seed)
    _w = jnp.asarray

    def _rec_inputs():
        import jax
        import jax.numpy as jnp
        _rk = jax.random.key(seed)
        x = -0.0002928 + 1 * jax.random.normal(jax.random.fold_in(_rk, 1), (64, 64, 256), jnp.float32)
        _lenS = 64 - jax.random.randint(jax.random.fold_in(_rk, 7), (64,), 0, max(1, 64 // 4) + 1, jnp.int32)
        _lenS2 = 64 - jax.random.randint(jax.random.fold_in(_rk, 8), (64,), 0, max(1, 64 // 4) + 1, jnp.int32)
        _ctx_2048P = jax.random.normal(jax.random.fold_in(_rk, 11), (64, 16, 256), jnp.float32)
        _ctx_2048c = jax.random.dirichlet(jax.random.fold_in(_rk, 511), 0.3 * jnp.ones((16,), jnp.float32), (64, 64))
        _ctx_2048t = jnp.einsum('bsk,bkd->bsd', _ctx_2048c, _ctx_2048P)
        _ctx_2048t = _ctx_2048t * jax.lax.rsqrt(jnp.mean(jnp.square(_ctx_2048t)) + 1e-12) * 0.953939
        ctx_2048 = -1.39393e-06 + 0.999914 * (_ctx_2048t + 0.3 * jax.random.normal(jax.random.fold_in(_rk, 611), (64, 64, 256), jnp.float32))
        return (x, ctx_2048)
    x, ctx_2048 = _rec_inputs()

    def _L0_xattn_setup():
        import math
        import jax, jax.numpy as jnp
        import numpy as np
        N_HEADS = 8
        CHANNELS = 64
        K_CH = CHANNELS // N_HEADS
        THETA = 10000.0

        def _rope_freqs(length, dim):
            inv_freq = 1.0 / THETA ** (jnp.arange(0, dim, 2, dtype=jnp.float32) / dim)
            f = jnp.arange(length, dtype=jnp.float32)[:, None] * inv_freq[None, :]
            return jnp.concatenate([f, f], axis=-1)

        def _apply_rotary(pos, t):
            half = t.shape[-1] // 2
            rot = jnp.concatenate([-t[..., half:], t[..., :half]], axis=-1)
            return t * jnp.cos(pos) + rot * jnp.sin(pos)

        def _proj(inp, W, b):
            return jnp.einsum('oc,bct->bot', W, inp) + b[None, :, None]
        key = jax.random.key(seed)
        ks = jax.random.split(key, 10)
        B, C, T = (4, CHANNELS, 256)
        bound = math.sqrt(6.0 / (C + C))

        def w(k):
            return jax.random.uniform(k, (C, C), jnp.float32, -bound, bound)
        return {'x': jax.random.normal(ks[0], (B, C, T), jnp.float32), 'c': jax.random.normal(ks[1], (B, C, T), jnp.float32), 'Wq': w(ks[2]), 'bq': jnp.zeros((C,), jnp.float32), 'Wk': w(ks[3]), 'bk': jnp.zeros((C,), jnp.float32), 'Wv': w(ks[4]), 'bv': jnp.zeros((C,), jnp.float32), 'Wo': w(ks[5]), 'bo': jnp.zeros((C,), jnp.float32)}
    _L0_xattn_all = _L0_xattn_setup()
    _L0_xattn_in = {k: v for k, v in _L0_xattn_all.items() if k in ('Wq', 'bq', 'Wk', 'bk', 'Wv', 'bv', 'Wo', 'bo')}
    del _L0_xattn_all

    def _L0_ffn_setup():
        import jax, jax.numpy as jnp
        import numpy as np
        H = 256
        I = 96
        E = 64
        TOP_K = 8
        B, S = (1, 128)
        key = jax.random.key(seed)
        ks = jax.random.split(key, 5)
        scale = 0.02
        return {'hidden_states': jax.random.normal(ks[0], (B, S, H), dtype=jnp.float32), 'W_router': jax.random.normal(ks[1], (H, E), dtype=jnp.float32) * scale, 'W_gate': jax.random.normal(ks[2], (E, H, I), dtype=jnp.float32) * scale, 'W_up': jax.random.normal(ks[3], (E, H, I), dtype=jnp.float32) * scale, 'W_down': jax.random.normal(ks[4], (E, I, H), dtype=jnp.float32) * scale}
    _L0_ffn_all = _L0_ffn_setup()
    _L0_ffn_in = {k: v for k, v in _L0_ffn_all.items() if k in ('W_router', 'W_gate', 'W_up', 'W_down')}
    del _L0_ffn_all

    def _L1_xattn_setup():
        import jax, jax.numpy as jnp
        import numpy as np
        H = 8
        D_MODEL = 64
        D_HEAD = D_MODEL // H
        key = jax.random.key(seed)
        ks = jax.random.split(key, 8)
        B, C, L = (4, D_MODEL, 256)
        s = 1.0 / np.sqrt(D_MODEL)
        return {'x1': jax.random.normal(ks[0], (B, C, L), dtype=jnp.float32), 'x2': jax.random.normal(ks[1], (B, C, L), dtype=jnp.float32), 'Wq': jax.random.uniform(ks[2], (D_MODEL, D_MODEL), jnp.float32, -s, s), 'bq': jax.random.uniform(ks[3], (D_MODEL,), jnp.float32, -s, s), 'Wk': jax.random.uniform(ks[4], (D_MODEL, D_MODEL), jnp.float32, -s, s), 'bk': jax.random.uniform(ks[5], (D_MODEL,), jnp.float32, -s, s), 'Wv': jax.random.uniform(ks[6], (D_MODEL, D_MODEL), jnp.float32, -s, s), 'bv': jax.random.uniform(ks[7], (D_MODEL,), jnp.float32, -s, s)}
    _L1_xattn_all = _L1_xattn_setup()
    _L1_xattn_in = {k: v for k, v in _L1_xattn_all.items() if k in ('Wq', 'bq', 'Wk', 'bk', 'Wv', 'bv')}
    del _L1_xattn_all

    def _L1_ffn_setup():
        import jax, jax.numpy as jnp
        import numpy as np
        B, S, D = (2, 256, 256)
        E, I, TOPK = (64, 96, 8)
        M = B * S
        CAP = 2 * (M * TOPK) // E

        def _moe(x, router_weight, gate_proj, up_proj, down_proj):
            b, s, d = x.shape
            xf = x.reshape(-1, d)
            m = xf.shape[0]
            logits = xf @ router_weight
            probs = jax.nn.softmax(logits.astype(jnp.float32), axis=-1)
            topw, topi = jax.lax.top_k(probs, TOPK)
            topw = topw / topw.sum(axis=-1, keepdims=True)
            flat_e = topi.reshape(-1)
            flat_w = topw.reshape(-1).astype(x.dtype)
            order = jnp.argsort(flat_e)
            se = flat_e[order]
            tok = order // TOPK
            counts = jax.ops.segment_sum(jnp.ones_like(flat_e), flat_e, num_segments=E)
            starts = jnp.cumsum(counts) - counts
            pos = jnp.arange(m * TOPK) - starts[se]
            valid = pos < CAP
            posc = jnp.minimum(pos, CAP - 1)
            xe = jnp.zeros((E, CAP, d), x.dtype).at[se, pos].set(xf[tok], mode='drop')
            h = jax.nn.silu(jnp.einsum('ecd,edi->eci', xe, gate_proj)) * jnp.einsum('ecd,edi->eci', xe, up_proj)
            ye = jnp.einsum('eci,eid->ecd', h, down_proj)
            contrib = jnp.where(valid[:, None], ye[se, posc], 0.0) * flat_w[order][:, None]
            out = jnp.zeros((m, d), x.dtype).at[tok].add(contrib)
            return out.reshape(b, s, d)
        key = jax.random.key(seed)
        k0, k1, k2, k3, k4 = jax.random.split(key, 5)
        return {'x': jax.random.normal(k0, (B, S, D), jnp.float32), 'router_weight': jax.random.normal(k1, (D, E), jnp.float32) * 0.02, 'gate_proj': jax.random.normal(k2, (E, D, I), jnp.float32) * 0.02, 'up_proj': jax.random.normal(k3, (E, D, I), jnp.float32) * 0.02, 'down_proj': jax.random.normal(k4, (E, I, D), jnp.float32) * 0.02}
    _L1_ffn_all = _L1_ffn_setup()
    _L1_ffn_in = {k: v for k, v in _L1_ffn_all.items() if k in ('router_weight', 'gate_proj', 'up_proj', 'down_proj')}
    del _L1_ffn_all
    return {'x': x, 'ctx_2048': ctx_2048, 'L0_xattn_Wq': _L0_xattn_in['Wq'], 'L0_xattn_bq': _L0_xattn_in['bq'], 'L0_xattn_Wk': _L0_xattn_in['Wk'], 'L0_xattn_bk': _L0_xattn_in['bk'], 'L0_xattn_Wv': _L0_xattn_in['Wv'], 'L0_xattn_bv': _L0_xattn_in['bv'], 'L0_xattn_Wo': _L0_xattn_in['Wo'], 'L0_xattn_bo': _L0_xattn_in['bo'], 'L0_ffn_W_router': _L0_ffn_in['W_router'], 'L0_ffn_W_gate': _L0_ffn_in['W_gate'], 'L0_ffn_W_up': _L0_ffn_in['W_up'], 'L0_ffn_W_down': _L0_ffn_in['W_down'], 'L1_xattn_Wq': _L1_xattn_in['Wq'], 'L1_xattn_bq': _L1_xattn_in['bq'], 'L1_xattn_Wk': _L1_xattn_in['Wk'], 'L1_xattn_bk': _L1_xattn_in['bk'], 'L1_xattn_Wv': _L1_xattn_in['Wv'], 'L1_xattn_bv': _L1_xattn_in['bv'], 'L1_ffn_router_weight': _L1_ffn_in['router_weight'], 'L1_ffn_gate_proj': _L1_ffn_in['gate_proj'], 'L1_ffn_up_proj': _L1_ffn_in['up_proj'], 'L1_ffn_down_proj': _L1_ffn_in['down_proj']}

def reference(x, ctx_2048, L0_xattn_Wq, L0_xattn_bq, L0_xattn_Wk, L0_xattn_bk, L0_xattn_Wv, L0_xattn_bv, L0_xattn_Wo, L0_xattn_bo, L0_ffn_W_router, L0_ffn_W_gate, L0_ffn_W_up, L0_ffn_W_down, L1_xattn_Wq, L1_xattn_bq, L1_xattn_Wk, L1_xattn_bk, L1_xattn_Wv, L1_xattn_bv, L1_ffn_router_weight, L1_ffn_gate_proj, L1_ffn_up_proj, L1_ffn_down_proj):
    import jax
    import jax.numpy as jnp

    def _L0_xattn_ref(x, c, Wq, bq, Wk, bk, Wv, bv, Wo, bo):
        import math
        import jax, jax.numpy as jnp
        import numpy as np
        N_HEADS = 8
        CHANNELS = 64
        K_CH = CHANNELS // N_HEADS
        THETA = 10000.0

        def _rope_freqs(length, dim):
            inv_freq = 1.0 / THETA ** (jnp.arange(0, dim, 2, dtype=jnp.float32) / dim)
            f = jnp.arange(length, dtype=jnp.float32)[:, None] * inv_freq[None, :]
            return jnp.concatenate([f, f], axis=-1)

        def _apply_rotary(pos, t):
            half = t.shape[-1] // 2
            rot = jnp.concatenate([-t[..., half:], t[..., :half]], axis=-1)
            return t * jnp.cos(pos) + rot * jnp.sin(pos)

        def _proj(inp, W, b):
            return jnp.einsum('oc,bct->bot', W, inp) + b[None, :, None]
        b, _, t_t = x.shape
        t_s = c.shape[2]
        q_emb = _rope_freqs(t_t, K_CH)
        k_emb = _rope_freqs(t_s, K_CH)

        def split_heads(t):
            return t.reshape(b, N_HEADS, K_CH, t.shape[2]).transpose(0, 1, 3, 2)
        q = split_heads(_proj(x, Wq, bq))
        k = split_heads(_proj(c, Wk, bk))
        v = split_heads(_proj(c, Wv, bv))
        q = _apply_rotary(q_emb, q)
        k = _apply_rotary(k_emb, k)
        scores = jnp.einsum('bhtc,bhsc->bhts', q, k) / math.sqrt(K_CH)
        p_attn = jax.nn.softmax(scores, axis=-1)
        out = jnp.einsum('bhts,bhsc->bhtc', p_attn, v)
        out = out.transpose(0, 1, 3, 2).reshape(b, N_HEADS * K_CH, t_t)
        return _proj(out, Wo, bo)

    def _L0_ffn_ref(hidden_states, W_router, W_gate, W_up, W_down):
        import jax, jax.numpy as jnp
        import numpy as np
        H = 256
        I = 96
        E = 64
        TOP_K = 8
        B, S = (1, 128)
        b, s, h = hidden_states.shape
        x = hidden_states.reshape(-1, h)
        logits = x @ W_router
        probs = jax.nn.softmax(logits.astype(jnp.float32), axis=-1)
        top_w, top_idx = jax.lax.top_k(probs, TOP_K)
        top_w = top_w / jnp.sum(top_w, axis=-1, keepdims=True)
        top_w = top_w.astype(x.dtype)
        comb = jnp.sum(jax.nn.one_hot(top_idx, E, dtype=x.dtype) * top_w[..., None], axis=1)
        g = jnp.einsum('th,ehi->eti', x, W_gate)
        u = jnp.einsum('th,ehi->eti', x, W_up)
        hmid = jax.nn.silu(g) * u
        hmid = hmid * comb.T[:, :, None]
        out = jnp.einsum('eti,eih->th', hmid, W_down)
        return out.reshape(b, s, h)

    def _L1_xattn_ref(x1, x2, Wq, bq, Wk, bk, Wv, bv):
        import jax, jax.numpy as jnp
        import numpy as np
        H = 8
        D_MODEL = 64
        D_HEAD = D_MODEL // H
        B, C, L = x1.shape
        x1t = jnp.swapaxes(x1, 1, 2)
        x2t = jnp.swapaxes(x2, 1, 2)

        def proj(x, W, b):
            y = jnp.einsum('blc,dc->bld', x, W) + b
            return y.reshape(B, -1, H, D_HEAD).transpose(0, 2, 1, 3)
        q = proj(x1t, Wq, bq)
        k = proj(x2t, Wk, bk)
        v = proj(x2t, Wv, bv)
        scores = jnp.einsum('bhqd,bhkd->bhqk', q, k) / jnp.sqrt(jnp.asarray(D_HEAD, dtype=q.dtype))
        attn = jax.nn.softmax(scores, axis=-1)
        out = jnp.einsum('bhqk,bhkd->bhqd', attn, v)
        out = out.transpose(0, 2, 1, 3).reshape(B, L, C)
        return jnp.swapaxes(out, 1, 2)

    def _L1_ffn_ref(x, router_weight, gate_proj, up_proj, down_proj):
        import jax, jax.numpy as jnp
        import numpy as np
        B, S, D = (2, 256, 256)
        E, I, TOPK = (64, 96, 8)
        M = B * S
        CAP = 2 * (M * TOPK) // E

        def _moe(x, router_weight, gate_proj, up_proj, down_proj):
            b, s, d = x.shape
            xf = x.reshape(-1, d)
            m = xf.shape[0]
            logits = xf @ router_weight
            probs = jax.nn.softmax(logits.astype(jnp.float32), axis=-1)
            topw, topi = jax.lax.top_k(probs, TOPK)
            topw = topw / topw.sum(axis=-1, keepdims=True)
            flat_e = topi.reshape(-1)
            flat_w = topw.reshape(-1).astype(x.dtype)
            order = jnp.argsort(flat_e)
            se = flat_e[order]
            tok = order // TOPK
            counts = jax.ops.segment_sum(jnp.ones_like(flat_e), flat_e, num_segments=E)
            starts = jnp.cumsum(counts) - counts
            pos = jnp.arange(m * TOPK) - starts[se]
            valid = pos < CAP
            posc = jnp.minimum(pos, CAP - 1)
            xe = jnp.zeros((E, CAP, d), x.dtype).at[se, pos].set(xf[tok], mode='drop')
            h = jax.nn.silu(jnp.einsum('ecd,edi->eci', xe, gate_proj)) * jnp.einsum('ecd,edi->eci', xe, up_proj)
            ye = jnp.einsum('eci,eid->ecd', h, down_proj)
            contrib = jnp.where(valid[:, None], ye[se, posc], 0.0) * flat_w[order][:, None]
            out = jnp.zeros((m, d), x.dtype).at[tok].add(contrib)
            return out.reshape(b, s, d)
        return _moe(x, router_weight, gate_proj, up_proj, down_proj)
    x = x + _L0_xattn_ref(_layernorm(x, axis=-1), ctx_2048, L0_xattn_Wq, L0_xattn_bq, L0_xattn_Wk, L0_xattn_bk, L0_xattn_Wv, L0_xattn_bv, L0_xattn_Wo, L0_xattn_bo)
    x = x + _L0_ffn_ref(_layernorm(x, axis=-1), L0_ffn_W_router, L0_ffn_W_gate, L0_ffn_W_up, L0_ffn_W_down)
    x = x + _L1_xattn_ref(_layernorm(x, axis=-1), ctx_2048, L1_xattn_Wq, L1_xattn_bq, L1_xattn_Wk, L1_xattn_bk, L1_xattn_Wv, L1_xattn_bv)
    x = x + _L1_ffn_ref(_layernorm(x, axis=-1), L1_ffn_router_weight, L1_ffn_gate_proj, L1_ffn_up_proj, L1_ffn_down_proj)
    return x

_drawn_inputs = setup_inputs


def setup_inputs(seed=0):
    import zlib

    import numpy as np

    out = dict(_drawn_inputs(seed))
    spreads = {'L0_xattn_bq': (0.0, 0.1),
     'L0_xattn_bk': (0.0, 0.68),
     'L0_xattn_bv': (0.0, 0.381),
     'L0_xattn_bo': (0.0, 0.326)}
    factors = {'L0_ffn_W_router': 8.0,
     'L0_ffn_W_gate': 8.0,
     'L0_ffn_W_up': 8.0,
     'L0_ffn_W_down': 8.0,
     'L1_xattn_bq': 26.152,
     'L1_xattn_bk': 64.0,
     'L1_ffn_router_weight': 8.0,
     'L1_ffn_gate_proj': 8.0,
     'L1_ffn_up_proj': 8.0,
     'L1_ffn_down_proj': 8.0,
     'L1_xattn_bv': 3.327}
    for name, (base, spread) in spreads.items():
        noise = np.random.default_rng([zlib.crc32(name.encode()), seed]).standard_normal(out[name].shape)
        drawn = base * np.exp(spread * noise) if base else spread * noise
        out[name] = jnp.asarray(drawn.astype(out[name].dtype))
    for name, factor in factors.items():
        out[name] = (out[name] * factor).astype(out[name].dtype)
    return out
```

```python
from contextlib import ExitStack

import numpy as np

import concourse.bass as bass
from concourse import mybir

F32 = mybir.dt.float32
BF16 = mybir.dt.bfloat16
I32 = mybir.dt.int32
U32 = mybir.dt.uint32
ALU = mybir.AluOpType
ACT = mybir.ActivationFunctionType
AX = mybir.AxisListType

P = 128
B, C, T = 64, 64, 256
NH, HC = 8, 8
PAIRS = B // 2
TOKENS = B * C
E, I, K = 64, 96, 8
CAP = 2 * (512 * K) // E
TILES0 = TOKENS * K // P + E
UNITS = 16
GROUPS = 4
TERMS_Q = ((0, 3), (1, 2), (2, 1))
TERMS_K = ((0, 3), (0, 2), (0, 1))
MAXROW = 48
SCALE = float(HC) ** -0.5
EPS = 1e-5
MAGIC = 1597463007.0
LISTLEN = E * TOKENS

LAG = dict(load=0, comb=1, front=2, stack=3, smax=4, attn=5, back=6, route=7, place=8, post=9)
STEPS = PAIRS + LAG["post"]
LOOP0, LOOPN = 10, 7
FB = 8
NB = 3

MISC = {
    0: [("mT1", "attn"), ("V", "smax"), ("OT0", "back"), ("OT1", "back"), ("Q", "front"),
        ("NT", "back"), ("K", "front"), ("mT0", "smax"), ("WO", "back"), ("XT", "route"),
        ("LG", "route"), ("RK", "route")],
    1: [("mT1", "attn"), ("V", "smax"), ("OT0", "back"), ("OT1", "back"), ("Q", "front"),
        ("NT", "back"), ("K", "front"), ("mT0", "smax"), ("LIST", "place"), ("XT", "route"),
        ("LG", "route"), ("RK", "route")],
}


class Step:

    def __init__(self, layer, s0, it=0):
        self.L, self.s0, self.it = layer, s0, it

    def on(self, stage):
        return 0 <= self.s0 - LAG[stage] < PAIRS

    def buf(self, stage):
        return (self.s0 - LAG[stage]) % NB

    def pair(self, stage):
        return self.s0 - LAG[stage] + self.it * 3

    def n(self, stage, per=1, extra=None):
        t0 = self.s0 - LAG[stage] + PAIRS * self.L
        extra = per if extra is None else extra
        return self.it * (3 * per) + (per * t0 + extra)

    def nbuf(self, stage, per=16):
        b = self.buf(stage)
        uses = len([t for t in range(PAIRS) if t % NB == b])
        t0 = self.s0 - LAG[stage]
        return self.it * per + per * (uses * self.L + t0 // NB + 1)

    def n1(self, stage, per=1, extra=None):
        extra = per if extra is None else extra
        return self.it * (3 * per) + (per * (self.s0 - LAG[stage]) + extra)

    def nbuf1(self, stage, per=16):
        return self.it * per + per * ((self.s0 - LAG[stage]) // NB + 1)

    def before(self, item):
        names = [name for name, _ in MISC[self.L]]
        i = names.index(item)
        bank, s = i % 2, self.s0
        while s >= 0:
            i -= 2
            if i < 0:
                i, s = i + len(names), s - 1
            if 0 <= s - LAG[MISC[self.L][i][1]] < PAIRS and s >= 0:
                return bank, MISC[self.L][i], Step(self.L, s, self.it)
        return bank, None, None


def steps(layer, engine, body):
    for s in range(LOOP0):
        body(Step(layer, s))
    with engine.Fori(0, LOOPN) as it:
        for c in range(NB):
            body(Step(layer, LOOP0 + c, it))
    for s in range(LOOP0 + NB * LOOPN, STEPS):
        body(Step(layer, s))


def row(t, n=P):
    return bass.ds(t * n, n)


def build(nc, x, ctx, tables, wts, out):
    stack = ExitStack()
    with stack:
        def sb(name, shape, dt=F32):
            return stack.enter_context(nc.sbuf_tensor(name, shape, dt))

        def sem(name):
            return stack.enter_context(nc.semaphore(name))

        def sems(name, n=NB):
            return [sem(f"{name}{i}") for i in range(n)]

        def dram(name, shape, dt=F32):
            return nc.dram_tensor(name, shape, dt).ap()

        stack_d = [dram(f"stack_d{b}", (2, 3, P, T), BF16) for b in range(NB)]
        x1_d = dram("x1_d", (TOKENS, T))
        x2_d = dram("x2_d", (TOKENS, T))
        xn_d = [dram("xn0_d", (TOKENS + P, T)), dram("xn1_d", (TOKENS + P, T + E))]
        list_d = dram("list_d", (LISTLEN, 1), I32)
        y0_d = dram("y0_d", (TILES0 * P, T))
        tile_d = dram("tile_d", (2, 3 * P), I32)

        psS = [stack.enter_context(nc.psum_tensor(f"psS{i}", [P, 512], F32)) for i in range(2)]
        psE = [stack.enter_context(nc.psum_tensor(f"psE{i}", [P, 512], F32)) for i in range(3)]
        psO = stack.enter_context(nc.psum_tensor("psO", [P, 512], F32))
        psM = [stack.enter_context(nc.psum_tensor(f"psM{i}", [P, 512], F32)) for i in range(2)]

        ident = sb("ident", [P, P])
        ones = sb("ones", [P, P], BF16)
        tri = sb("tri", [P, P], BF16)
        iota_e = sb("iota_e", [P, E])
        iota_r = sb("iota_r", [P, P], BF16)
        iota_i = sb("iota_i", [P, P], I32)
        part1 = sb("part1", [P, 1])
        base0 = sb("base0", [P, E])
        one_row = sb("one_row", [P, T], BF16)
        total = sb("total", [P, E])
        id_acc = sb("id_acc", [P, E])
        tok0 = sb("tok0", [P, 1])
        tokf = sb("tokf", [P, 1])

        part_i = sb("part_i", [P, 1], I32)
        slot_i = sb("slot_i", [P, 3], I32)
        base_i = sb("base_i", [P, E], I32)
        slotk = sb("slotk", [P, 3])
        spare = sb("spare", [P, 1])
        top_all = sb("top_all", [P, PAIRS * K])
        place_all = sb("place_all", [P, PAIRS * K])
        row_all = sb("row_all", [P, PAIRS * K], I32)
        w_all = sb("w_all", [P, PAIRS * K])
        idx_e = sb("idx_e", [P, E], I32)

        wbd1 = {n: sb(f"proj_{n}1", [P, P]) for n in "qkv"}
        bias = sb("bias", [P, 7])
        bv = [sb(f"bv{L}", [P, 2 * P]) for L in range(2)]
        wr = [sb(f"router{L}", [P, 2, E]) for L in range(2)]

        zrow = sb("zrow", [2, 8 * T], BF16)
        mv = sb("mv", [P, 2, 2])

        att = ExitStack()

        def ab(name, shape, dt=F32):
            return att.enter_context(nc.sbuf_tensor(name, shape, dt))

        cos = ab("cos", [P, T])
        sin = ab("sin", [P, T])
        wbd = [{n: ab(f"proj_{n}0", [P, P]) for n in "qrksvo"}, wbd1]
        wcmp = ab("wcmp", [P, 9, C])
        xin = [ab(f"xin{b}", [P, T]) for b in range(NB)]
        x2 = [ab(f"x2_{b}", [P, T]) for b in range(NB)]
        ctx_t = [ab(f"ctx{b}", [P, T]) for b in range(NB)]
        xres = [ab(f"xres{b}", [P, T]) for b in range(NB)]
        xn = [ab(f"xn{b}", [P, T]) for b in range(NB)]
        rope = ab("rope", [P, 2, 2, T])
        qk = [ab(f"qk{b}", [P, 2, T]) for b in range(NB)]
        rem = ab("rem", [P, 2, T])
        parts = [ab(f"parts{b}", [P, 2, 3, T], BF16) for b in range(NB)]
        q2 = [ab(f"q2_{b}", [P, 8, T], BF16) for b in range(NB)]
        k2 = [ab(f"k2_{b}", [P, 8, 2 * T], BF16) for b in range(NB)]
        mx = [ab(f"mx{b}", [P, 2, 16]) for b in range(NB)]
        mhi = [ab(f"mhi{h}", [P, 2, 8], BF16) for h in range(2)]
        msp = [ab(f"msp{h}", [P, 2, 2, 8]) for h in range(2)]
        mrow = [ab(f"mrow{h}", [32, P], BF16) for h in range(2)]
        v = [ab(f"v{b}", [P, 2, UNITS, 32]) for b in range(NB)]
        prob = [ab(f"prob{g}", [P, 4, 512]) for g in range(3)]
        osb = ab("osb", [P, GROUPS, T])
        rec = ab("rec", [P, 2, UNITS])
        nrm = ab("nrm", [P, 2, P])
        nt = ab("nt", [P, T])
        x1 = [ab(f"x1_{b}", [P, T]) for b in range(NB)]
        stats = ab("stats", [P, 2, 6])
        nwt = ab("nwt", [P, 6, 2])
        rstd = ab("rstd", [P, 2])
        xr = [ab(f"xr{b}", [P, T + E]) for b in range(NB)]
        xT = ab("xT", [P, 2, P])
        logit = ab("logit", [P, E])
        rest = ab("rest", [P, E])
        top = [ab(f"top{b}", [P, 8]) for b in range(NB)]
        topi = [ab(f"topi{b}", [P, 8], U32) for b in range(NB)]
        topf = [ab(f"topf{b}", [P, 8]) for b in range(NB)]
        mask = [ab(f"mask{b}", [P, E], BF16) for b in range(NB)]
        ntop = ab("ntop", [P, 1])
        ex = ab("ex", [P, E])
        exm = ab("exm", [P, E])
        den = ab("den", [P, 2])
        place = ab("place", [P, E])
        hot = ab("hot", [P, K, E])
        posf = [ab(f"posf{b}", [P, K]) for b in range(NB)]
        posi = [ab(f"posi{b}", [P, K], I32) for b in range(NB)]
        toki = [ab(f"toki{b}", [P, 1], I32) for b in range(NB)]
        hotr = ab("hotr", [P, K, P], BF16)
        hote = ab("hote", [P, 2, K, E], BF16)
        posb = [ab(f"posb{b}", [P, K], I32) for b in range(NB)]
        yg = ab("yg", [P, K, T])
        zinit = ab("zinit", [P, LISTLEN // P], I32)
        zf = ab("zf", [P, T + E])
        att.close()

        ffn = ExitStack()

        def fb(name, shape, dt=F32):
            return ffn.enter_context(nc.sbuf_tensor(name, shape, dt))

        gu = fb("gu", [P, E, 2, 2 * I])
        dn = fb("dn", [I, E, T])
        xg = [fb(f"xg{b}", [P, T + E]) for b in range(FB)]
        idx = [fb(f"idx{b}", [P, 1], I32) for b in range(FB)]
        xgT = [fb(f"xgT{b}", [P, 2, P]) for b in range(2)]
        sil = [fb(f"sil{b}", [P, I]) for b in range(2)]
        hid = [fb(f"hid{b}", [P, I]) for b in range(2)]
        hT = [fb(f"hT{b}", [I, P]) for b in range(2)]
        y_all = fb("y_all", [P, FB, T])
        y = [y_all[:, b, :] for b in range(FB)]
        idx_s = [fb(f"idx_s{b}", [P, 1], I32) for b in range(FB)]
        wcol = [fb(f"wcol{b}", [P, 1]) for b in range(FB)]
        cnt = fb("cnt", [P, 6, E])
        cnti = fb("cnti", [P, E], I32)
        fhot = y_all[:, 0:2, :].rearrange("p a (b e) -> p (a b) e", e=E)
        rowd = fb("rowd", [P, PAIRS * K])
        cumT = fb("cumT", [E, P])
        tri_f = fb("tri_f", [E, E])
        cmp_ = fb("cmp_", [P, 3, E])
        cmpm = fb("cmpm", [P, 3, E])
        owner = fb("owner", [P, 4, 3])
        tab = fb("tab", [P, 2, 3], I32)
        tabrow = fb("tabrow", [1, 2, TILES0], I32)
        ffn.close()

        s_bar = sem("s_bar")
        s_pool_set, s_vec_set = sem("s_pool_set"), sem("s_vec_set")
        s_clear = sem("s_clear")
        d_small, d_setup, d_ones = sem("d_small"), sem("d_setup"), sem("d_ones")
        d_x, d_ctx, d_xres = sems("d_x"), sems("d_ctx"), sems("d_xres")
        d_parts, d_stack = sems("d_parts"), sems("d_stack")
        d_max = [sems("d_maxa"), sems("d_maxb")]
        d_x2, d_x1, d_xn, d_list = sems("d_x2"), sems("d_x1"), sems("d_xn"), sems("d_list")
        d_yg = sem("d_yg")
        s_comb = sem("s_comb")
        s_mvx, s_mvr, s_rstd = sem("s_mvx"), sem("s_mvr"), sem("s_rstd")
        s_xn, s_xr = sem("s_xn"), sem("s_xr")
        s_qp, s_kp, s_qr, s_kr, s_qk = (sem(n) for n in ("s_qp", "s_kp", "s_qr", "s_kr", "s_qk"))
        s_p1, s_rem, s_p2, s_p3 = (sem(n) for n in ("s_p1", "s_rem", "s_p2", "s_p3"))
        s_score, s_max = sem("s_score"), sem("s_max")
        s_msp, s_mT, s_mrow = sems("s_msp", 2), sems("s_mT", 2), sems("s_mrow", 2)
        s_st, s_exp = sem("s_st"), sem("s_exp")
        s_pv, s_oev = sem("s_pv"), sem("s_oev")
        s_vp, s_v = sem("s_vp"), sem("s_v")
        s_ot, s_nrm = sems("s_ot", 2), sems("s_nrm", 2)
        s_ntp, s_nt, s_wo, s_x1 = (sem(n) for n in ("s_ntp", "s_nt", "s_wo", "s_x1"))
        s_xtp, s_xT, s_lgp, s_logit = (sem(n) for n in ("s_xtp", "s_xT", "s_lgp", "s_logit"))
        s_top, s_topf, s_ntop, s_mask, s_rkp = (sem(n) for n in ("s_top", "s_topf", "s_ntop", "s_mask", "s_rkp"))
        s_place, s_tot, s_ex, s_wk, s_wall = (sem(n) for n in ("s_place", "s_tot", "s_ex", "s_wk", "s_wall"))
        s_hot, s_posf, s_posi, s_lhs, s_lsp, s_list = (
            sem(n) for n in ("s_hot", "s_posf", "s_posi", "s_lhs", "s_lsp", "s_list"))
        s_posb, s_fhot = sem("s_posb"), sem("s_fhot")
        s_chain = sem("s_chain")
        s_held = sem("s_held")
        d_w, d_tab = sem("d_w"), sem("d_tab")
        s_r1, s_r2, s_r3 = sem("s_r1"), sem("s_r2"), sem("s_r3")
        d_idx, d_xg, d_y = sems("d_idx", FB), sems("d_xg", FB), sems("d_y", FB)
        s_idx, s_xp, s_xgT, s_gup, s_sil, s_hid, s_hp, s_hT, s_yp, s_y, s_wcol = (
            sem(n) for n in ("s_idx", "s_xp", "s_xgT", "s_gup", "s_sil", "s_hid", "s_hp", "s_hT",
                             "s_yp", "s_y", "s_wcol"))
        d_acc = sem("d_acc")

        block = stack.enter_context(nc.Block())

        def barrier(eng, k):
            eng.drain().then_inc(s_bar, 1)
            eng.wait_ge(s_bar, 5 * k)

        def wait(eng, semaphore, value):
            if not isinstance(value, int) or value > 0:
                eng.wait_ge(semaphore, value)

        def hold(eng, semaphore, value):
            wait(eng, semaphore, value)
            if not isinstance(value, int):
                eng.sem_inc(s_held, 1)

        def uses_of(b):
            return len([t for t in range(PAIRS) if t % NB == b])

        def last(st, stage, per=1, back=1):
            return st.n(stage, per, per * (1 - back))

        def lastbuf(st, stage, per=16):
            return st.nbuf(stage, per) - per

        FREE = dict(mT0=s_mrow[0], mT1=s_mrow[1], V=s_v, OT0=s_nrm[0], OT1=s_nrm[1], Q=s_qr, K=s_kr,
                    NT=s_nt, WO=s_x1, XT=s_xT, LG=s_logit, RK=s_tot, LIST=s_list)

        def bank(pe, st, item):
            at, before, then = st.before(item)
            if before:
                name, stage = before
                if name == "LIST":
                    pe.wait_ge(s_list, then.n1(stage))
                elif name == "NT" and st.L == 1:
                    pe.wait_ge(s_x1, then.n(stage))
                else:
                    pe.wait_ge(FREE[name], then.n(stage))
            return psM[at]

        def head_cols(tile, o, n):
            return tile[:, :].rearrange("p (h r) -> p h r", r=32)[:, :, o:o + n]

        def item_bank(L, name):
            return [n for n, _ in MISC[L]].index(name) % 2

        FLAG = dict(idx=0, gather=4, X=8, GU=9, H=10, D=11)
        JOBS = (TILES0, E)

        class Slot:

            def __init__(self, layer, s0, it=0):
                self.L, self.s0, self.it = layer, s0, it

            def on(self, stage):
                return 0 <= self.s0 - FLAG[stage] < JOBS[self.L]

            def job(self, stage):
                return self.s0 - FLAG[stage] + self.it * FB

            def buf(self, stage, n=FB):
                return (self.s0 - FLAG[stage]) % n

            def n(self, stage, back=0):
                return self.it * FB + (self.s0 - FLAG[stage] + 1 - back + (JOBS[0] if self.L else 0))

            def nbuf(self, stage, back=0):
                return self.it * 16 + 16 * ((self.s0 - FLAG[stage]) // FB + 1 - back
                                            + (JOBS[0] // FB if self.L else 0))

            def nbuf0(self, stage, back=0):
                return self.it * 16 + 16 * ((self.s0 - FLAG[stage]) // FB + 1 - back)

        def slots(layer, eng, body, look_up=None):
            def group(first, n, it=0):
                table = look_up(Slot(layer, first, it)) if look_up else None
                for c in range(n):
                    body(Slot(layer, first + c, it), table)

            end = JOBS[layer] + FLAG["D"]
            group(0, FB)
            group(FB, FB)
            with eng.Fori(0, JOBS[layer] // FB - 2) as it:
                group(2 * FB, FB, it)
            for s in range(JOBS[layer], end, FB):
                group(s, min(FB, end - s))

        def look_up(engine, column, first_stage, last_stage):
            def read(st):
                lo, hi = st.s0 - FLAG[first_stage], st.s0 + FB - 1 - FLAG[last_stage]
                if isinstance(st.it, int):
                    lo, hi = max(lo, 0), min(hi, TILES0 - 1)
                if hi < lo:
                    return {}
                most = (LISTLEN - P, E - 1)[column]
                _, values = nc.values_load_multi_w_load_instructions(
                    tabrow[0:1, column, bass.ds(lo + st.it * FB, hi - lo + 1)], engines=(engine,),
                    min_val=0, max_val=most, skip_runtime_bounds_check_because="the table is clamped")
                return {lo + i: value for i, value in enumerate(values)}
            return read

        def sp_slot(st, first_row):
            sp = nc.sync
            if st.on("idx"):
                b = st.buf("idx")
                hold(sp, d_xg[b], st.nbuf0("idx", 1))
                sp.dma_start(idx[b][:, :], list_d[bass.ds(first_row[st.s0 - FLAG["idx"]], P), :])\
                  .then_inc(d_idx[b], 16)
            if st.on("D"):
                b = st.buf("D")
                hold(sp, s_y, st.n("D"))
                sp.dma_start(y0_d[row(st.job("D")), :], y[b]).then_inc(d_y[b], 16)

        @block.sync
        def _(sp):
            loads = [(cos[:, :], tables[0]), (sin[:, :], tables[1]), (bias[:, :], wts["bias"]),
                     (bv[0][:, :], wts["bv0"]), (bv[1][:, :], wts["bv1"]),
                     (wr[0][:, :, :], wts["wr0"]), (wr[1][:, :, :], wts["wr1"]),
                     (wcmp[0:C, :, :], wts["small"]), (wcmp[C:P, :, :], wts["small"])]
            for dst, src in loads:
                sp.dma_start(dst, src).then_inc(d_small, 16)
            def ones_rows(L):
                sp.wait_ge(s_clear, L + 1)
                for b in range(NB):
                    for hh in range(2):
                        for g in range(8):
                            sp.dma_start(k2[b][64 * hh + MAXROW:64 * hh + MAXROW + 2, g, hh * T:(hh + 1) * T],
                                         one_row[0:2, :]).then_inc(d_ones, 16)
                sp.wait_ge(d_ones, 16 * 16 * NB * (L + 1))

            sp.wait_ge(s_pool_set, 1)
            sp.dma_start(list_d.rearrange("(p n) o -> p (n o)", p=P), zinit[:, :]).then_inc(d_setup, 16)
            sp.dma_start(xn_d[0][TOKENS:TOKENS + P, :], zf[:, 0:T]).then_inc(d_setup, 16)
            sp.dma_start(xn_d[1][TOKENS:TOKENS + P, :], zf[:, :]).then_inc(d_setup, 16)
            sp.dma_start(out[TOKENS:TOKENS + P, :], zf[:, 0:T]).then_inc(d_setup, 16)
            ones_rows(0)
            sp.wait_ge(d_setup, 16 * 4)
            barrier(sp, 1)

            def body(st):
                L = st.L
                if st.on("load"):
                    b, t = st.buf("load"), st.pair("load")
                    hold(sp, s_xn, last(st, "load", back=NB))
                    sp.dma_start(xin[b][:, :], (x, x1_d)[L][row(t), :]).then_inc(d_x[b], 16)
                if st.on("attn"):
                    b, t = st.buf("attn"), st.pair("attn")
                    hold(sp, s_x1, last(st, "attn", back=NB))
                    if L == 1:
                        hold(sp, d_x2[b], st.nbuf1("attn"))
                    sp.dma_start(xres[b][:, :], (x, x2_d)[L][row(t), :]).then_inc(d_xres[b], 16)
                if st.on("post") and L == 1:
                    b, t = st.buf("post"), st.pair("post")
                    hold(sp, s_wall, st.n1("post"))
                    sp.dma_start(xn_d[1][row(t), :], xr[b][:, :]).then_inc(d_xn[b], 16)
                if st.on("attn"):
                    b = st.buf("attn")
                    hold(sp, s_mrow[1], st.n("attn"))
                    for hh in range(2):
                        sp.dma_start(q2[b][64 * hh + MAXROW:64 * hh + MAXROW + 2, 4:8, :].rearrange("p g t -> p (g t)"),
                                     mrow[1][16 * hh:16 * hh + 16, :]).then_inc(d_max[1][b], 16)
                if st.on("stack"):
                    b = st.buf("stack")
                    hold(sp, s_p3, st.n("stack"))
                    hold(sp, d_stack[b], lastbuf(st, "stack", 16 * 14))
                    sp.dma_start(stack_d[b].rearrange("q a p t -> p (q a) t"),
                                 parts[b][:, :, :, :].rearrange("p q a t -> p (q a) t")).then_inc(d_parts[b], 16)
                if st.on("comb"):
                    b, t = st.buf("comb"), st.pair("comb")
                    hold(sp, s_vp, last(st, "comb", back=NB))
                    sp.dma_start(ctx_t[b][:, :], ctx[row(t), :]).then_inc(d_ctx[b], 16)
                if st.on("stack"):
                    b = st.buf("stack")
                    hold(sp, s_st, last(st, "stack", UNITS, back=NB))
                    hold(sp, d_parts[b], st.nbuf("stack"))
                    for hh in range(2):
                        r = 64 * hh
                        for (part, n), (kpart, kn) in zip(TERMS_Q, TERMS_K):
                            src = stack_d[b][0, part, 64 * hh:64 * hh + 64, :]
                            sp.dma_start(q2[b][r:r + 8 * n, :, :],
                                         bass.AP(src.tensor, src.offset, [[0, n], [8 * T, 8], [T, 8], [1, T]]))\
                              .then_inc(d_stack[b], 16)
                            src = stack_d[b][1, kpart, 64 * hh:64 * hh + 64, :]
                            sp.dma_start(k2[b][r:r + 8 * n, :, hh * T:(hh + 1) * T],
                                         bass.AP(src.tensor, src.offset, [[P * T, n], [8 * T, 8], [T, 8], [1, T]]))\
                              .then_inc(d_stack[b], 16)
                            r += 8 * n
                        sp.dma_start(q2[b][r:r + 2, :, :].rearrange("p g t -> p (g t)"), zrow[:, :])\
                          .then_inc(d_stack[b], 16)
                if st.on("route") and L == 0:
                    b, t = st.buf("route"), st.pair("route")
                    hold(sp, s_xr, st.n("route"))
                    sp.dma_start(xn_d[0][row(t), :], xr[b][:, 0:T]).then_inc(d_xn[b], 16)
                if st.on("comb") and L == 1:
                    b, t = st.buf("comb"), st.pair("comb")
                    hold(sp, s_comb, st.n1("comb", K))
                    sp.dma_start(x2_d[row(t), :], x2[b][:, :]).then_inc(d_x2[b], 16)
                if st.on("smax"):
                    b = st.buf("smax")
                    hold(sp, s_mrow[0], st.n("smax"))
                    for hh in range(2):
                        sp.dma_start(q2[b][64 * hh + MAXROW:64 * hh + MAXROW + 2, 0:4, :].rearrange("p g t -> p (g t)"),
                                     mrow[0][16 * hh:16 * hh + 16, :]).then_inc(d_max[0][b], 16)
                if st.on("back"):
                    b, t = st.buf("back"), st.pair("back")
                    hold(sp, s_x1, st.n("back"))
                    sp.dma_start((x1_d, out)[L][row(t), :], x1[b][:, :]).then_inc(d_x1[b], 16)

            for L in range(2):
                if L == 1:
                    ones_rows(1)
                    barrier(sp, 4)
                steps(L, sp, body)
                for b in range(NB):
                    sp.wait_ge(d_x1[b], 16 * (L + 1) * uses_of(b))
                    sp.wait_ge(d_xn[b], 16 * (L + 1) * uses_of(b))
                barrier(sp, 2 + 3 * L)
                for c in range(8):
                    es = slice(8 * c, 8 * c + 8)
                    sp.dma_start(gu[:, es, :, :], wts["gu"][L][:, es, :, :]).then_inc(d_w, 16)
                    sp.dma_start(dn[:, es, :], wts["dn"][L][:, es, :]).then_inc(d_w, 16)
                if L == 0:
                    sp.wait_ge(s_r3, 1)
                    for w in range(2):
                        sp.dma_start(tile_d[w].rearrange("(c p) -> p c", p=P), tab[:, w, :],
                                     allow_slow_non_contiguous=True).then_inc(d_tab, 16)
                    sp.wait_ge(d_tab, 32)
                    sp.dma_start(tabrow[0:1, :, :], tile_d.rearrange("w (o n) -> o w n", o=1)[:, :, 0:TILES0]).then_inc(d_tab, 16)
                    sp.wait_ge(d_tab, 48)
                    slots(L, sp, sp_slot, look_up(mybir.EngineType.SP, 0, "idx", "idx"))
                    for b in range(FB):
                        sp.wait_ge(d_y[b], 16 * TILES0 // FB)
                barrier(sp, 3 + 3 * L)

        @block.gpsimd
        def _(pool):
            g = nc.gpsimd

            def set_up(ins):
                ins.then_inc(s_pool_set, 1)

            g.memset(ident[:, :], 0.0)
            g.memset(zf[:, :], 0.0)
            g.memset(zrow[:, :], 0.0)
            g.memset(one_row[:, :], 1.0)
            g.memset(zinit[:, :], TOKENS)
            g.iota(iota_i[:, :], [[1, P]], base=0, channel_multiplier=0)
            pool.drain().then_inc(s_pool_set, 1)
            pool.wait_ge(s_pool_set, 1)
            g.affine_select(out=ident[:, :], in_=ident[:, :], compare_op=ALU.not_equal, fill=1.0,
                            base=0, pattern=[[-1, P]], channel_multiplier=1)
            g.affine_select(out=tri[:, :], in_=one_row[:, 0:P], compare_op=ALU.is_gt, fill=0.0,
                            base=0, pattern=[[1, P]], channel_multiplier=-1)
            g.iota(part_i[:, 0:1], [[0, 1]], base=0, channel_multiplier=1)
            g.iota(slot_i[:, :], [[P, 3]], base=0, channel_multiplier=1)
            g.iota(base_i[:, :], [[TOKENS, E]], base=0, channel_multiplier=0)
            pool.drain().then_inc(s_pool_set, 1)
            barrier(pool, 1)

            def body(st):
                L = st.L
                if st.on("front") or st.on("route"):
                    hold(pool, s_rstd, st.it * 3 + (st.s0 - 1 + L * (STEPS - 4)))
                if st.on("front"):
                    b = st.buf("front")
                    hold(pool, s_qp, last(st, "front", back=NB))
                    g.tensor_scalar(xn[b][:, :], (xin, x2)[L][b][:, :], mv[:, 0, 0:1], rstd[:, 0:1],
                                    ALU.subtract, ALU.mult).then_inc(s_xn, 1)
                if st.on("route"):
                    b = st.buf("route")
                    hold(pool, d_xn[b], lastbuf(st, "route"))
                    g.tensor_scalar(xr[b][:, 0:T], x1[b][:, :], mv[:, 1, 0:1], rstd[:, 1:2],
                                    ALU.subtract, ALU.mult).then_inc(s_xr, 1)
                if L == 1 and st.on("load"):
                    b = st.buf("load")
                    hold(pool, s_posb, st.n1("load"))
                    hold(pool, s_comb, st.n1("load", K, 0))
                    for k in range(K):
                        g.indirect_dma_start(yg[:, k, :], None, y0_d[:, :],
                                             bass.IndirectOffsetOnAxis(posb[b][:, k:k + 1], 0)).then_inc(d_yg, 16)
                if L == 0 and st.on("post"):
                    b = st.buf("post")
                    hold(pool, s_posi, st.n1("post"))
                    for k in range(K):
                        g.indirect_dma_start(list_d[:, :], bass.IndirectOffsetOnAxis(posi[b][:, k:k + 1], 0),
                                             toki[b][:, 0:1], None).then_inc(d_list[b], 16)
                if st.on("front"):
                    b = st.buf("front")
                    if L == 0:
                        hold(pool, s_qr, st.n("front"))
                        hold(pool, s_kr, st.n("front"))
                        g.tensor_tensor(qk[b][:, :, :], rope[:, 0, :, :], rope[:, 1, :, :], ALU.add).then_inc(s_qk, 1)
                        hold(pool, s_qk, st.n("front"))
                    hold(pool, s_p1, st.n("front"))
                    if L == 1:
                        hold(pool, s_kr, st.n("front"))
                    g.tensor_tensor(rem[:, :, :], qk[b][:, :, :], parts[b][:, :, 0, :], ALU.subtract).then_inc(s_rem, 1)
                    hold(pool, s_p2, st.n("front"))
                    hold(pool, s_rem, st.n("front"))
                    g.tensor_tensor(parts[b][:, :, 2, :], rem[:, :, :], parts[b][:, :, 1, :], ALU.subtract).then_inc(s_p3, 1)

            def slot_body(st, table):
                L = st.L
                if st.on("gather"):
                    b = st.buf("gather")
                    if L == 0:
                        hold(pool, d_idx[b], st.nbuf0("gather"))
                    else:
                        hold(pool, s_idx, st.n("gather") - JOBS[0])
                    hold(pool, s_xp, st.n("gather", FB))
                    if L == 1:
                        hold(pool, s_wcol, st.n("gather", FB) - JOBS[0])
                    g.indirect_dma_start(xg[b][:, 0:(T, T + E)[L]], None, xn_d[L][:, :],
                                         bass.IndirectOffsetOnAxis(idx[b][:, 0:1], 0)).then_inc(d_xg[b], 16)
                if st.on("D") and L == 1:
                    b = st.buf("D")
                    hold(pool, s_y, st.n("D"))
                    hold(pool, d_acc, (st.job("D")) * 16)
                    g.indirect_dma_start(out[:, :], bass.IndirectOffsetOnAxis(idx_s[b][:, 0:1], 0),
                                         y[b], None, compute_op=ALU.add).then_inc(d_acc, 16)

            for L in range(2):
                if L == 1:
                    barrier(pool, 4)
                steps(L, pool, body)
                if L == 0:
                    for b in range(NB):
                        pool.wait_ge(d_list[b], 16 * K * uses_of(b))
                barrier(pool, 2 + 3 * L)
                if L == 1:
                    pool.wait_ge(s_r2, 3)
                slots(L, pool, slot_body)
                if L == 1:
                    pool.wait_ge(d_acc, 16 * E)
                barrier(pool, 3 + 3 * L)

        @block.scalar
        def _(act):
            a = nc.scalar
            barrier(act, 1)

            def body(st):
                L = st.L

                def o_out(stage, q):
                    if not st.on(stage):
                        return
                    act.wait_ge(s_pv, st.n(stage, 4, q + 1))
                    if q == 0:
                        wait(act, s_ot[1], last(st, stage))
                    a.copy(osb[:, q, :], psO[:, (q % 2) * T:(q % 2 + 1) * T]).then_inc(s_oev, 1)

                for u in range(UNITS):
                    if st.on("attn"):
                        act.wait_ge(s_st, st.n("attn", UNITS, u + 1))
                        if u % 4 == 0:
                            wait(act, s_pv, st.n("attn", 4, u // 4 - 2))
                        gr = (4 * (st.s0 - LAG["attn"]) + u // 4) % 3
                        ring = (UNITS * (st.s0 - LAG["attn"]) + u) % 3
                        a.activation(prob[gr][:, u % 4, :], psE[ring][:, :], ACT.Exp, scale=SCALE).then_inc(s_exp, 1)
                    if u == 0:
                        o_out("back", 2)
                    if u == 4:
                        o_out("back", 3)
                    if u == 8:
                        o_out("attn", 0)
                    if u == 12:
                        o_out("attn", 1)
                    if u == 1 and st.on("place"):
                        b = st.buf("place")
                        act.wait_ge(s_ntop, st.n("place"))
                        wait(act, s_wk if L == 0 else s_wall, st.n1("place", 1, 0))
                        if L == 0:
                            a.activation(ex[:, 0:K], top[b][:, :], ACT.Exp, bias=ntop[:, 0:1]).then_inc(s_ex, 1)
                        else:
                            a.activation(ex[:, :], logit[:, :], ACT.Exp, bias=ntop[:, 0:1]).then_inc(s_ex, 1)
                    if L == 1 and u in (7, 9) and st.on("front"):
                        b, i = st.buf("front"), (u - 7) // 2
                        act.wait_ge((s_qp, s_kp)[i], st.n("front"))
                        wait(act, s_rem, last(st, "front", back=NB))
                        a.activation(qk[b][:, i, :], psM[item_bank(1, "QK"[i])][:, 0:T], ACT.Identity,
                                     bias=bias[:, 5 + i:6 + i]).then_inc((s_qr, s_kr)[i], 1)
                    if L == 0 and u == 9 and st.on("back"):
                        act.wait_ge(s_ntp, st.n("back"))
                        wait(act, s_wo, last(st, "back"))
                        a.copy(nt[:, :], psM[item_bank(0, "NT")][:, 0:T]).then_inc(s_nt, 1)
                    if u == 12 and st.on("route"):
                        act.wait_ge(s_xtp, st.n("route"))
                        wait(act, s_lgp, last(st, "route"))
                        a.copy(xT[:, :, :].rearrange("p c t -> p (c t)"), psM[item_bank(L, "XT")][:, 0:2 * P]).then_inc(s_xT, 1)
                    if u == 13 and st.on("route"):
                        act.wait_ge(s_lgp, st.n("route"))
                        wait(act, s_mask, last(st, "route"))
                        wait(act, s_ex, last(st, "route"))
                        a.copy(logit[:, :], psM[item_bank(L, "LG")][:, 0:E]).then_inc(s_logit, 1)

            def slot_body(st, table):
                if st.on("X"):
                    act.wait_ge(s_xp, st.n("X"))
                    wait(act, s_gup, st.n("X", 2))
                    a.copy(xgT[st.buf("X", 2)][:, :, :].rearrange("p c t -> p (c t)"),
                           psS[st.buf("X", 2)][:, 0:2 * P]).then_inc(s_xgT, 1)
                if st.on("GU"):
                    act.wait_ge(s_gup, st.n("GU"))
                    wait(act, s_hid, st.n("GU", 2))
                    a.activation(sil[st.buf("GU", 2)][:, :], psE[st.buf("GU", 2)][:, 0:I], ACT.Silu).then_inc(s_sil, 1)
                if st.on("D") and st.L == 0:
                    act.wait_ge(s_yp, st.n("D"))
                    wait(act, d_y[st.buf("D")], st.nbuf0("D", 1))
                    a.copy(y[st.buf("D")], psM[st.buf("D", 2)][:, 0:T]).then_inc(s_y, 1)

            for L in range(2):
                if L == 1:
                    barrier(act, 4)
                steps(L, act, body)
                barrier(act, 2 + 3 * L)
                slots(L, act, slot_body)
                barrier(act, 3 + 3 * L)

        @block.vector
        def _(dve):
            v_ = nc.vector

            class Chain:
                n, it, per = 0, 0, 0

                def add(self, ins):
                    ins.then_inc(s_chain, 1)
                    self.n += 1

                def join(self):
                    if isinstance(self.it, int):
                        dve.wait_ge(s_chain, self.n)
                    else:
                        hold(dve, s_chain, self.it * self.per + self.n)

            ch = Chain()

            def clear(L):
                for b in range(NB):
                    v_.memset(q2[b][:, :, :], 0.0)
                    v_.memset(k2[b][:, :, :], 0.0)
                    v_.memset(v[b][:, :, :, :], 0.0)
                dve.drain().then_inc(s_clear, 1)
                dve.wait_ge(s_clear, L + 1)
                for b in range(NB):
                    v_.memset(v[b][:, :, :, 8:9], 1.0)

            clear(0)
            v_.memset(mv[:, :, :], 1.0)
            v_.memset(ones[:, :], 1.0)
            v_.memset(id_acc[:, :], 0.0)
            v_.memset(tok0[:, :], 0.0)
            for w in wbd:
                for tile in w.values():
                    v_.memset(tile[:, :], 0.0)
            dve.drain().then_inc(s_vec_set, 1)
            dve.wait_ge(s_vec_set, 1)
            dve.wait_ge(s_pool_set, 2)
            v_.tensor_copy(iota_e[:, :], iota_i[:, 0:E])
            v_.tensor_copy(iota_r[:, :], iota_i[:, :])
            v_.tensor_copy(tokf[:, :], part_i[:, :])
            v_.tensor_copy(slotk[:, :], slot_i[:, :])
            v_.tensor_copy(base0[:, :], base_i[:, :])
            v_.tensor_copy(total[:, :], base_i[:, :])
            v_.tensor_scalar(part1[:, :], part_i[:, :], 1.0, None, ALU.add)
            dve.drain().then_inc(s_vec_set, 2)
            dve.wait_ge(d_small, 16 * 9)
            place_of = [(0, n) for n in "qrksvo"] + [(1, n) for n in "qkv"]
            for i, (L, n) in enumerate(place_of):
                for b in range(2):
                    rows = slice(C * b, C * b + C)
                    if n in "vo":
                        dst, src = wbd[L][n][rows, C * b:C * b + C], wcmp[rows, i, :]
                    else:
                        dst = wbd[L][n][rows, :].rearrange("p (r b g) -> p r b g", b=2, g=4)[:, :, b, :]
                        src = wcmp[rows, i, :].rearrange("p (r g) -> p r g", g=4)
                    v_.tensor_copy(dst, src)
            barrier(dve, 1)

            def newton(i):
                ve, y0, t1, t2 = nwt[:, 0, :], nwt[:, 1, :], nwt[:, 2, :], nwt[:, 3, :]
                ch.join()
                if i == 0:
                    ch.add(v_.tensor_scalar(ve, mv[:, :, 1], EPS, None, ALU.add))
                elif i == 1:
                    ch.add(v_.tensor_scalar(y0.bitcast(I32), ve.bitcast(I32), -0.5, MAGIC, ALU.mult, ALU.add))
                elif i % 3 == 2:
                    ch.add(v_.tensor_tensor(t1, ve, y0, ALU.mult))
                elif i % 3 == 0:
                    ch.add(v_.scalar_tensor_tensor(t2, t1, -0.5, y0, ALU.mult, ALU.mult))
                elif i < 10:
                    ch.add(v_.scalar_tensor_tensor(y0, t2, 1.5, y0, ALU.add, ALU.mult))
                else:
                    v_.scalar_tensor_tensor(rstd[:, :], t2, 1.5, y0, ALU.add, ALU.mult).then_inc(s_rstd, 1)

            def body(st):
                L, it = st.L, st.it

                def red(u):
                    b = st.buf("smax")
                    bg, tt = u // 2, u % 2
                    dve.wait_ge(s_score, st.n("smax", UNITS, u + 1))
                    v_.tensor_reduce(mx[b][:, bg // 4, :].rearrange("p (h r) -> p h r", h=2)[:, :, (bg % 4) * 2 + tt],
                                     psS[u % 2][:, :].rearrange("p (h s) -> p h s", h=2), AX.X, ALU.max)\
                      .then_inc(s_max, 1)

                def split_max(h):
                    b = st.buf("smax")
                    m = mx[b][:, h, :].rearrange("p (h r) -> p h r", h=2)
                    dve.wait_ge(s_max, st.n("smax", UNITS, 8 * h + 8))
                    ch.add(v_.tensor_scalar(mhi[h][:, :, :], m, -1.0, None, ALU.mult))
                    wait(dve, s_mT[h], last(st, "smax"))
                    ch.join()
                    v_.tensor_copy(msp[h][:, :, 0, :], mhi[h][:, :, :]).then_inc(s_msp[h], 1)
                    v_.scalar_tensor_tensor(msp[h][:, :, 1, :], m, -1.0, mhi[h][:, :, :], ALU.mult, ALU.subtract)\
                      .then_inc(s_msp[h], 1)

                def max_rows(stage, h):
                    dve.wait_ge(s_mT[h], st.n(stage))
                    wait(dve, d_max[h][(st.s0 - LAG[stage] - 1) % NB], Step(L, st.s0 - 1, it).nbuf(stage, 32)
                         if st.s0 - 1 >= LAG[stage] else 0)
                    v_.tensor_copy(mrow[h][:, :], psM[item_bank(L, f"mT{h}")][0:32, 0:P]).then_inc(s_mrow[h], 1)

                def normalise(h):
                    ps = psM[item_bank(L, f"OT{h}")]
                    dve.wait_ge(s_ot[h], st.n("back"))
                    ch.add(v_.reciprocal(rec[:, h, :], head_cols(ps, 8, 1).rearrange("p h o -> p (h o)")))
                    wait(dve, s_ntp, last(st, "back"))
                    ch.join()
                    r = rec[:, h, :]
                    v_.tensor_tensor(nrm[:, h, :].rearrange("p (h c) -> p h c", c=HC), head_cols(ps, 0, HC),
                                     bass.AP(r.tensor, r.offset, [list(r.ap[0]), [1, UNITS], [0, HC]]),
                                     ALU.mult).then_inc(s_nrm[h], 1)

                def rotate(i):
                    b = st.buf("front")
                    ps = psM[item_bank(0, "QK"[i])]
                    dve.wait_ge((s_qp, s_kp)[i], st.n("front"))
                    wait(dve, s_qk, last(st, "front"))
                    v_.scalar_tensor_tensor(rope[:, 0, i, :], ps[:, 0:T], bias[:, 2 * i:2 * i + 1], cos[:, :],
                                            ALU.add, ALU.mult)
                    v_.scalar_tensor_tensor(rope[:, 1, i, :], ps[:, T:2 * T], bias[:, 2 * i + 1:2 * i + 2], sin[:, :],
                                            ALU.add, ALU.mult).then_inc((s_qr, s_kr)[i], 1)

                for u in range(UNITS):
                    if st.on("smax"):
                        red(u)
                    if u == 0 and L == 1 and st.on("load"):
                        hold(dve, d_yg, st.n1("load", 16 * K, 0) - 32 * K)
                        v_.tensor_copy(posb[st.buf("load")][:, :], row_all[:, row(st.pair("load"), K)])\
                          .then_inc(s_posb, 1)
                    if u == 0 and st.on("place"):
                        dve.wait_ge(s_rkp, st.n("place"))
                        wait(dve, s_tot, st.n("place", 1, 0))
                        wait(dve, s_hot, last(st, "place"))
                        v_.tensor_tensor(place[:, :], psM[item_bank(L, "RK")][:, 0:E], total[:, :], ALU.add)\
                          .then_inc(s_place, 1)
                        dve.wait_ge(s_place, st.n("place"))
                        v_.tensor_tensor(total[:, :], psM[item_bank(L, "RK")][:, E:2 * E], total[:, :], ALU.add)\
                          .then_inc(s_tot, 1)
                    if u == 1 and st.on("place"):
                        b = st.buf("place")
                        dve.wait_ge(s_topf, st.n("place"))
                        dve.wait_ge(s_place, st.n("place"))
                        for k in range(K):
                            ins = v_.scalar_tensor_tensor(hot[:, k, :], iota_e[:, :], topf[b][:, k:k + 1],
                                                          place[:, :], ALU.is_equal, ALU.mult)
                        ins.then_inc(s_hot, 1)
                    if L == 1 and u < K and st.on("comb"):
                        b = st.buf("comb")
                        if u == 0:
                            dve.wait_ge(d_yg, st.n1("comb", 16 * K))
                            dve.wait_ge(d_x[b], st.nbuf("comb"))
                            wait(dve, d_x2[b], st.nbuf1("comb") - 16)
                        else:
                            dve.wait_ge(s_comb, st.n1("comb", K, u))
                        v_.scalar_tensor_tensor(x2[b][:, :], yg[:, u, :],
                                                w_all[:, bass.ds(st.pair("comb") * K + u, 1)],
                                                (x2 if u else xin)[b][:, :], ALU.mult, ALU.add).then_inc(s_comb, 1)
                    if u <= 5 and (st.on("front") or st.on("route")):
                        if u == 0:
                            if st.on("front"):
                                dve.wait_ge(s_mvx, st.n("front"))
                            if st.on("route"):
                                dve.wait_ge(s_mvr, st.n("route"))
                        newton(2 * u)
                        if u < 5:
                            newton(2 * u + 1)
                    if u == 1 and st.on("attn"):
                        max_rows("attn", 1)
                    if u == 4 and st.on("smax"):
                        b = st.buf("smax")
                        dve.wait_ge(s_vp, st.n("smax"))
                        wait(dve, s_pv, last(st, "smax", 4, back=NB))
                        v_.tensor_tensor(v[b][:, :, :, 0:HC],
                                         psM[item_bank(L, "V")][:, 0:2 * P].rearrange("p (s h c) -> p s h c", s=2, c=HC),
                                         bv[L][:, :].rearrange("p (s h c) -> p s h c", s=2, c=HC), ALU.add)\
                          .then_inc(s_v, 1)
                    if u == 2 and st.on("place"):
                        dve.wait_ge(s_ex, st.n("place"))
                        if L == 0:
                            ch.add(v_.tensor_reduce(den[:, 0:1], ex[:, 0:K], AX.X, ALU.add))
                        else:
                            ch.add(v_.tensor_tensor(exm[:, :], ex[:, :], mask[st.buf("place")][:, :], ALU.mult))
                    if u == 3 and st.on("place") and L == 1:
                        ch.join()
                        ch.add(v_.tensor_reduce(den[:, 0:1], exm[:, :], AX.X, ALU.add))
                    if u == 4 and st.on("place"):
                        ch.join()
                        ch.add(v_.reciprocal(den[:, 1:2], den[:, 0:1]))
                    if u == 5 and st.on("place"):
                        b = st.buf("place")
                        ch.join()
                        if L == 0:
                            v_.tensor_scalar(w_all[:, row(st.pair("place"), K)], ex[:, 0:K], den[:, 1:2], None, ALU.mult).then_inc(s_wk, 1)
                        else:
                            v_.tensor_scalar(xr[b][:, T:T + E], exm[:, :], den[:, 1:2], None, ALU.mult)\
                              .then_inc(s_wall, 1)
                    if u == 5 and st.on("back"):
                        normalise(0)
                    if u == 6 and st.on("back"):
                        normalise(1)
                    if u == 6 and st.on("place") and L == 0:
                        b = st.buf("place")
                        hold(dve, d_list[b], st.nbuf1("place", 16 * K) - 16 * K)
                        ch.join()
                        ch.add(v_.tensor_copy(toki[b][:, :], tokf[:, :]))
                        ch.join()
                        ch.add(v_.tensor_scalar(tokf[:, :], tokf[:, :], float(P), None, ALU.add))
                    if L == 0 and u == 7 and st.on("front"):
                        rotate(0)
                    if L == 0 and u == 9 and st.on("front"):
                        rotate(1)
                    if u == 8 and st.on("smax"):
                        split_max(0)
                    if L == 1 and u == 8 and st.on("back"):
                        b = st.buf("back")
                        dve.wait_ge(s_ntp, st.n("back"))
                        dve.wait_ge(d_xres[b], st.nbuf("back"))
                        wait(dve, d_x1[b], lastbuf(st, "back"))
                        v_.tensor_tensor(x1[b][:, :], psM[item_bank(1, "NT")][:, 0:T], xres[b][:, :], ALU.add)\
                          .then_inc(s_x1, 1)
                    if u == 6 and st.on("place") and L == 1:
                        b = st.buf("place")
                        wait(dve, s_lsp, st.n1("place", 1, 0))
                        for k in range(K):
                            v_.tensor_scalar(hote[:, 0, k, :], iota_e[:, :], topf[b][:, k:k + 1], None, ALU.is_equal)
                        ch.add(v_.tensor_copy(spare[:, :], ntop[:, :]))
                        ch.join()
                        v_.tensor_scalar(hote[:, 1, :, :], hote[:, 0, :, :], part1[:, 0:1], None, ALU.mult)
                    if u == 8 and st.on("place"):
                        b = st.buf("place")
                        hold(dve, s_hot, st.n("place"))
                        if L == 1:
                            v_.tensor_reduce(posf[b][:, :], hot[:, :, :], AX.X, ALU.add).then_inc(s_posf, 1)
                        else:
                            here = row(st.pair("place"), K)
                            v_.tensor_reduce(place_all[:, here], hot[:, :, :], AX.X, ALU.add).then_inc(s_posf, 1)
                            v_.tensor_copy(top_all[:, here], topf[b][:, :])
                            hold(dve, s_posf, st.n("place"))
                            v_.tensor_copy(posi[b][:, :], place_all[:, here]).then_inc(s_posi, 1)
                    if u == 9 and st.on("place") and L == 1:
                        b = st.buf("place")
                        dve.wait_ge(s_posf, st.n("place"))
                        for k in range(K):
                            ins = v_.tensor_scalar(hotr[:, k, :], iota_r[:, :], posf[b][:, k:k + 1], None, ALU.is_equal)
                        ins.then_inc(s_lhs, 1)
                    if u == 10 and st.on("smax"):
                        max_rows("smax", 0)
                    if L == 0 and u == 11 and st.on("back"):
                        b = st.buf("back")
                        dve.wait_ge(s_wo, st.n("back"))
                        dve.wait_ge(d_xres[b], st.nbuf("back"))
                        wait(dve, d_x1[b], lastbuf(st, "back"))
                        v_.scalar_tensor_tensor(x1[b][:, :], psM[item_bank(0, "WO")][:, 0:T], bias[:, 4:5], xres[b][:, :],
                                                ALU.add, ALU.add).then_inc(s_x1, 1)
                    if L == 1 and u == 12 and st.on("place"):
                        ps = psM[item_bank(1, "LIST")]
                        dve.wait_ge(s_lsp, st.n1("place"))
                        ch.join()
                        ch.add(v_.scalar_tensor_tensor(id_acc[:, :], ps[:, 0:E], tok0[:, 0:1], id_acc[:, :],
                                                       ALU.mult, ALU.add))
                        ch.join()
                        ch.add(v_.tensor_scalar(tok0[:, :], tok0[:, :], float(P), None, ALU.add))
                        v_.tensor_tensor(id_acc[:, :], ps[:, E:2 * E], id_acc[:, :], ALU.add).then_inc(s_list, 1)
                        dve.wait_ge(s_list, st.n1("place"))
                    if u == 12 and st.on("front"):
                        b = st.buf("front")
                        dve.wait_ge(s_qk if L == 0 else s_kr, st.n("front"))
                        wait(dve, d_parts[b], lastbuf(st, "front"))
                        v_.tensor_copy(parts[b][:, :, 0, :], qk[b][:, :, :]).then_inc(s_p1, 1)
                    if u == 13 and st.on("route"):
                        b = st.buf("route")
                        hold(dve, s_logit, st.n("route"))
                        v_.max(top[b][:, :], logit[:, :]).then_inc(s_top, 1)
                    if u == 14 and st.on("route"):
                        b = st.buf("route")
                        hold(dve, s_top, st.n("route"))
                        hold(dve, s_ex, last(st, "route"))
                        v_.max_index(topi[b][:, :], top[b][:, :], logit[:, :])
                        v_.tensor_scalar(ntop[:, :], top[b][:, 0:1], -1.0, None, ALU.mult).then_inc(s_ntop, 1)
                        ch.add(v_.match_replace(rest[:, :], top[b][:, :], logit[:, :], -3.0e38))
                        ch.join()
                        v_.tensor_tensor(mask[b][:, :], rest[:, :], logit[:, :], ALU.not_equal).then_inc(s_mask, 1)
                        v_.tensor_copy(topf[b][:, :], topi[b][:, :]).then_inc(s_topf, 1)
                    if u == 14 and st.on("back"):
                        b = st.buf("back")
                        dve.wait_ge(s_x1, st.n("back"))
                        wait(dve, s_xr, last(st, "back"))
                        v_.bn_stats(stats[:, 1, :], x1[b][:, :])
                        ch.add(v_.tensor_copy(spare[:, :], tokf[:, :]))
                        ch.join()
                        v_.bn_aggr(mv[:, 1, :], stats[:, 1, :]).then_inc(s_mvr, 1)
                    if u == 15 and st.on("comb"):
                        b = st.buf("comb")
                        if L == 0:
                            dve.wait_ge(d_x[b], st.nbuf("comb"))
                        else:
                            dve.wait_ge(s_comb, st.n1("comb", K))
                        v_.bn_stats(stats[:, 0, :], (xin, x2)[L][b][:, :])
                        wait(dve, s_xn, last(st, "comb"))
                        ch.add(v_.tensor_copy(spare[:, :], tokf[:, :]))
                        ch.join()
                        v_.bn_aggr(mv[:, 0, :], stats[:, 0, :]).then_inc(s_mvx, 1)
                    if u == 15 and st.on("front"):
                        b = st.buf("front")
                        dve.wait_ge(s_rem, st.n("front"))
                        v_.tensor_copy(parts[b][:, :, 1, :], rem[:, :, :]).then_inc(s_p2, 1)
                    if u == 15 and st.on("smax"):
                        split_max(1)

            def run(L):
                for s in range(LOOP0):
                    before = ch.n
                    body(Step(L, s))
                ch.per = 3 * (ch.n - before)
                with dve.Fori(0, LOOPN) as it:
                    ch.it = it
                    before = ch.n
                    for c in range(NB):
                        body(Step(L, LOOP0 + c, it))
                    assert ch.n - before == ch.per
                ch.it = 0
                ch.n += ch.per * (LOOPN - 1)
                for s in range(LOOP0 + NB * LOOPN, STEPS):
                    body(Step(L, s))

            def link(ins):
                ch.add(ins)
                ch.join()

            def tiles_table():
                link(v_.tensor_tensor(cnt[:, 0, :], total[:, :], base0[:, :], ALU.subtract))
                link(v_.tensor_scalar(cnti[:, :], cnt[:, 0, :], float(P - 1), None, ALU.add))
                link(v_.tensor_scalar(cnti[:, :], cnti[:, :], 7, None, ALU.logical_shift_right))
                link(v_.tensor_copy(cnt[:, 1, :], cnti[:, :]))
                v_.tensor_scalar(cnt[:, 2, :], cnt[:, 1, :], 1.0, None, ALU.max).then_inc(s_r1, 1)
                link(v_.tensor_scalar(tri_f[:, :], iota_e[0:E, :], part1[0:E, 0:1], None, ALU.subtract))
                link(v_.tensor_scalar(tri_f[:, :], tri_f[:, :], -1.0, None, ALU.is_ge))
                dve.wait_ge(s_r2, 1)
                v_.tensor_copy(cumT[:, :], psM[0][0:E, 0:P]).then_inc(s_r1, 1)
                dve.wait_ge(s_r2, 2)
                link(v_.tensor_copy(cnt[:, 3, :], psM[1][:, 0:E]))
                link(v_.tensor_scalar(owner[:, 0, :], slotk[:, :], cnt[:, 3, E - 1:E], None, ALU.is_ge))
                link(v_.scalar_tensor_tensor(slotk[:, :], owner[:, 0, :], -float(TOKENS * K // P), slotk[:, :],
                                             ALU.mult, ALU.add))
                for c in range(3):
                    link(v_.tensor_scalar(cmp_[:, c, :], cnt[:, 3, :], slotk[:, c:c + 1], None, ALU.is_le))
                    link(v_.tensor_tensor(cmpm[:, c, :], cmp_[:, c, :], cnt[:, 3, :], ALU.mult))
                link(v_.tensor_reduce(owner[:, 0, :], cmp_[:, :, :], AX.X, ALU.add))
                link(v_.tensor_reduce(owner[:, 1, :], cmpm[:, :, :], AX.X, ALU.max))
                link(v_.tensor_tensor(owner[:, 2, :], slotk[:, :], owner[:, 1, :], ALU.subtract))
                link(v_.tensor_scalar(owner[:, 3, :], owner[:, 2, :], float(P), None, ALU.mult))
                link(v_.scalar_tensor_tensor(owner[:, 3, :], owner[:, 0, :], float(TOKENS), owner[:, 3, :],
                                             ALU.mult, ALU.add))
                link(v_.tensor_copy(tab[:, 0, :], owner[:, 3, :]))
                link(v_.tensor_scalar(owner[:, 0, :], owner[:, 0, :], float(E - 1), None, ALU.min))
                v_.tensor_copy(tab[:, 1, :], owner[:, 0, :]).then_inc(s_r3, 1)
                link(v_.tensor_tensor(cnt[:, 4, :], cnt[:, 3, :], cnt[:, 2, :], ALU.subtract))
                link(v_.scalar_tensor_tensor(cnt[:, 5, :], cnt[:, 4, :], float(P), base0[:, :],
                                             ALU.mult, ALU.subtract))
                done = ch.n
                with dve.Fori(0, PAIRS) as t:
                    hold(dve, s_chain, t * 1 + done)
                    for k in range(K):
                        ins = v_.scalar_tensor_tensor(fhot[:, k, :], iota_e[:, :], top_all[:, bass.ds(t * K + k, 1)],
                                                      cnt[:, 5, :], ALU.is_equal, ALU.mult)
                    ins.then_inc(s_fhot, 1)
                    hold(dve, s_fhot, t + 1)
                    v_.tensor_reduce(rowd[:, row(t, K)], fhot[:, :, :], AX.X, ALU.add).then_inc(s_chain, 1)
                ch.n += PAIRS
                ch.join()
                link(v_.tensor_tensor(rowd[:, :], rowd[:, :], place_all[:, :], ALU.add))
                link(v_.tensor_copy(row_all[:, :], rowd[:, :]))

            def lists():
                link(v_.tensor_scalar(cnt[:, 0, :], id_acc[:, :], 0.0, None, ALU.is_equal))
                link(v_.tensor_scalar(cnt[:, 1, :], id_acc[:, :], -1.0, None, ALU.add))
                link(v_.tensor_scalar(cnt[:, 2, 0:1], part1[:, :], float(TOKENS), None, ALU.add))
                link(v_.scalar_tensor_tensor(cnt[:, 3, :], cnt[:, 0, :], cnt[:, 2, 0:1], cnt[:, 1, :],
                                             ALU.mult, ALU.add))
                v_.tensor_copy(idx_e[:, :], cnt[:, 3, :]).then_inc(s_r2, 1)
                dve.wait_ge(s_r2, 3)

            def slot_body(st, table):
                L = st.L
                if L == 1 and st.on("idx"):
                    b = st.buf("idx")
                    hold(dve, d_xg[b], st.nbuf("idx", 1))
                    v_.tensor_copy(idx[b][:, :], idx_e[:, bass.ds(st.job("idx"), 1)]).then_inc(s_idx, 1)
                if L == 1 and st.on("X"):
                    b = st.buf("X")
                    hold(dve, s_y, st.n("X", FB))
                    hold(dve, d_xg[b], st.nbuf("X"))
                    v_.tensor_copy(wcol[b][:, :], xg[b][:, bass.ds(st.job("X") + T, 1)]).then_inc(s_wcol, 1)
                if st.on("GU"):
                    i = st.buf("GU", 2)
                    dve.wait_ge(s_sil, st.n("GU"))
                    wait(dve, s_hp, st.n("GU", 2))
                    v_.tensor_tensor(hid[i][:, :], sil[i][:, :], psE[i][:, I:2 * I], ALU.mult).then_inc(s_hid, 1)
                if st.on("H"):
                    i = st.buf("H", 2)
                    dve.wait_ge(s_hp, st.n("H"))
                    wait(dve, s_yp, st.n("H", 2))
                    v_.tensor_copy(hT[i][:, :], (psE[2], psO)[i][0:I, 0:P]).then_inc(s_hT, 1)
                if L == 1 and st.on("D"):
                    b = st.buf("D")
                    hold(dve, s_yp, st.n("D"))
                    hold(dve, d_acc, (st.job("D") - 3) * 16)
                    v_.tensor_copy(idx_s[b][:, :], idx_e[:, bass.ds(st.job("D"), 1)])
                    dve.wait_ge(s_wcol, st.n("D") - JOBS[0])
                    v_.tensor_scalar(y[b], psM[st.buf("D", 2)][:, 0:T], wcol[b][:, 0:1], None, ALU.mult)\
                      .then_inc(s_y, 1)

            for L in range(2):
                if L == 1:
                    clear(1)
                    barrier(dve, 4)
                run(L)
                barrier(dve, 2 + 3 * L)
                if L == 0:
                    tiles_table()
                else:
                    lists()
                slots(L, dve, slot_body)
                if L == 0:
                    link(v_.memset(total[:, :], 0.0))
                barrier(dve, 3 + 3 * L)

        @block.tensor
        def _(pe):
            m_ = nc.tensor
            barrier(pe, 1)

            def body(st):
                L = st.L

                def scores(u):
                    b, bg, tt = st.buf("smax"), u // 2, u % 2
                    if u == 0:
                        pe.wait_ge(d_stack[b], st.nbuf("smax", 16 * 14))
                    wait(pe, s_max, st.n("smax", UNITS, u - 1))
                    m_.matmul(psS[u % 2][:, :], q2[b][:, bg, tt * P:(tt + 1) * P], k2[b][:, bg, :],
                              start=True, stop=True).then_inc(s_score, 1)

                def scores_t(u):
                    b, bg, hh = st.buf("attn"), u // 2, u % 2
                    if u % 8 == 0:
                        pe.wait_ge(d_max[u // 8][b], st.nbuf("attn", 32))
                    wait(pe, s_exp, st.n("attn", UNITS, u - 2))
                    ring = (UNITS * (st.s0 - LAG["attn"]) + u) % 3
                    for i in range(2):
                        ins = m_.matmul(psE[ring][:, i * T:(i + 1) * T],
                                        k2[b][:, bg, hh * T + i * P:hh * T + (i + 1) * P], q2[b][:, bg, :],
                                        start=True, stop=True)
                    ins.then_inc(s_st, 1)

                def values(stage, q):
                    if not st.on(stage):
                        return
                    b = st.buf(stage)
                    gr = (4 * (st.s0 - LAG[stage]) + q) % 3
                    pe.wait_ge(s_exp, st.n(stage, UNITS, 4 * q + 4))
                    pe.wait_ge(s_v, st.n(stage))
                    wait(pe, s_oev, st.n(stage, 4, q))
                    for i in range(2):
                        for j in range(4):
                            ins = m_.matmul(psO[32 * j:32 * j + 32, (q % 2) * T:(q % 2 + 1) * T],
                                            v[b][:, i, 4 * q + j, :], prob[gr][:, j, i * T:(i + 1) * T],
                                            start=(i == 0), stop=(i == 1))
                    ins.then_inc(s_pv, 1)

                def product(item, stage, ready, terms, done, n=T):
                    for semaphore, value in ready:
                        pe.wait_ge(semaphore, value)
                    ps = bank(pe, st, item)
                    for i, (lhs, rhs) in enumerate(terms):
                        if rhs is None:
                            w = lhs.shape[1] if len(lhs.shape) == 2 else 32
                            ins = m_.transpose(ps[0:w, i * P:(i + 1) * P], lhs, ident[:, :])
                        else:
                            ins = m_.matmul(ps[:, i * n:(i + 1) * n], lhs, rhs, start=True, stop=True)
                    ins.then_inc(done, 1)

                for u in range(UNITS):
                    if st.on("smax"):
                        scores(u)
                    if st.on("attn"):
                        scores_t(u)
                    if u == 3:
                        values("back", 3)
                    if u in (7, 11, 15):
                        values("attn", (u - 7) // 4)
                    if u == 1 and st.on("attn"):
                        product("mT1", "attn", [(s_msp[1], st.n("attn", 2))],
                                [(msp[1][:, :, :, :].rearrange("p h a r -> p (h a r)"), None)], s_mT[1])
                    if u == 4 and st.on("smax"):
                        b = st.buf("smax")
                        product("V", "smax", [(d_ctx[b], st.nbuf("smax"))],
                                [(ctx_t[b][:, i * P:(i + 1) * P], wbd[L]["v"][:, :]) for i in range(2)], s_vp, P)
                    if u in (5, 6) and st.on("back"):
                        h = u - 5
                        product(f"OT{h}", "back", [(s_oev, st.n("back", 4))],
                                [(osb[:, q, h * P:(h + 1) * P], None) for q in range(GROUPS)], s_ot[h])
                    if u == 7 and st.on("front"):
                        b = st.buf("front")
                        product("Q", "front", [(s_xn, st.n("front"))],
                                [(wbd[L][n][:, :], xn[b][:, :]) for n in ("qr", "q")[L]], s_qp)
                    if u == 8 and st.on("back"):
                        product("NT", "back", [(s_nrm[0], st.n("back")), (s_nrm[1], st.n("back"))],
                                [(nrm[:, h, :], None) for h in range(2)], s_ntp)
                    if u == 9 and st.on("front"):
                        b = st.buf("front")
                        product("K", "front", [(d_ctx[b], st.nbuf("front"))],
                                [(wbd[L][n][:, :], ctx_t[b][:, :]) for n in ("ks", "k")[L]], s_kp)
                    if u == 10 and st.on("smax"):
                        product("mT0", "smax", [(s_msp[0], st.n("smax", 2))],
                                [(msp[0][:, :, :, :].rearrange("p h a r -> p (h a r)"), None)], s_mT[0])
                    if u == 11 and st.on("back") and L == 0:
                        product("WO", "back", [(s_nt, st.n("back"))], [(wbd[0]["o"][:, :], nt[:, :])], s_wo)
                    if u == 11 and st.on("place") and L == 1:
                        pe.wait_ge(s_lhs, st.n1("place"))
                        ps = bank(pe, st, "LIST")
                        for k in range(K):
                            ins = m_.matmul(ps[:, 0:2 * E], hotr[:, k, :], hote[:, :, k, :],
                                            start=(k == 0), stop=(k == K - 1))
                        ins.then_inc(s_lsp, 1)
                    if u == 12 and st.on("route"):
                        b = st.buf("route")
                        product("XT", "route", [(s_xr, st.n("route"))],
                                [(xr[b][:, i * P:(i + 1) * P], None) for i in range(2)], s_xtp)
                    if u == 13 and st.on("route"):
                        pe.wait_ge(s_xT, st.n("route"))
                        ps = bank(pe, st, "LG")
                        for i in range(2):
                            ins = m_.matmul(ps[:, 0:E], xT[:, i, :], wr[L][:, i, :], start=(i == 0), stop=(i == 1))
                        ins.then_inc(s_lgp, 1)
                    if u == 15 and st.on("route"):
                        b = st.buf("route")
                        product("RK", "route", [(s_mask, st.n("route"))],
                                [(tri[:, :], mask[b][:, :]), (ones[:, :], mask[b][:, :])], s_rkp, E)

            def slot_body(st, table):
                if st.on("X"):
                    b, i = st.buf("X"), st.buf("X", 2)
                    pe.wait_ge(d_xg[b], st.nbuf("X"))
                    for c in range(2):
                        ins = m_.transpose(psS[i][:, c * P:(c + 1) * P], xg[b][:, c * P:(c + 1) * P], ident[:, :])
                    ins.then_inc(s_xp, 1)
                if st.on("GU"):
                    i = st.buf("GU", 2)
                    pe.wait_ge(s_xgT, st.n("GU"))
                    for c in range(2):
                        ins = m_.matmul(psE[i][:, 0:2 * I], xgT[i][:, c, :],
                                        gu[:, bass.ds(expert(st, "GU", table), 1), c, :].rearrange("p o n -> p (o n)"),
                                        start=(c == 0), stop=(c == 1))
                    ins.then_inc(s_gup, 1)
                if st.on("H"):
                    i = st.buf("H", 2)
                    pe.wait_ge(s_hid, st.n("H"))
                    m_.transpose((psE[2], psO)[i][0:I, 0:P], hid[i][:, :], ident[:, :]).then_inc(s_hp, 1)
                if st.on("D"):
                    i = st.buf("D", 2)
                    pe.wait_ge(s_hT, st.n("D"))
                    wait(pe, s_y, st.n("D", 2))
                    m_.matmul(psM[i][:, 0:T], hT[i][:, :],
                              dn[:, bass.ds(expert(st, "D", table), 1), :].rearrange("p o n -> p (o n)"),
                              start=True, stop=True).then_inc(s_yp, 1)

            def expert(st, stage, table):
                return st.job(stage) if st.L == 1 else table[st.s0 - FLAG[stage]]

            for L in range(2):
                if L == 1:
                    barrier(pe, 4)
                steps(L, pe, body)
                barrier(pe, 2 + 3 * L)
                if L == 0:
                    pe.wait_ge(s_r1, 1)
                    m_.transpose(psM[0][0:E, 0:P], cnt[:, 2, :], ident[:, :]).then_inc(s_r2, 1)
                    pe.wait_ge(s_r1, 2)
                    m_.matmul(psM[1][:, 0:E], cumT[:, :], tri_f[:, :], start=True, stop=True).then_inc(s_r2, 1)
                    pe.wait_ge(d_tab, 48)
                pe.wait_ge(d_w, 16 * 16 * (L + 1))
                slots(L, pe, slot_body, None if L else look_up(mybir.EngineType.PE, 1, "D", "GU"))
                barrier(pe, 3 + 3 * L)


def rotary_tables():
    half = HC // 2
    inv = (np.float32(1.0) / np.float32(10000.0) ** (np.arange(0, HC, 2, dtype=np.float32) / np.float32(HC)))
    pos = np.arange(T, dtype=np.float32)[:, None] * inv.astype(np.float32)[None, :]
    c = np.cos(pos.astype(np.float64)).astype(np.float32).T
    s = np.sin(pos.astype(np.float64)).astype(np.float32).T
    cos = np.concatenate([c, c])
    sin = np.concatenate([-s, s])
    return tuple(np.ascontiguousarray(np.broadcast_to(a[None, :, None, :], (2, HC, 8, T)).reshape(P, T))
                 for a in (cos, sin))


def kernel(**inputs):
    import concourse.bacc as bacc
    from concourse.bass_utils import run_bass_kernel_spmd

    a = {n: np.asarray(z) for n, z in inputs.items()}

    def stacked(w, roll=0):
        w = np.roll(w.reshape(4, 2, HC, -1), roll, axis=2)
        return w.transpose(3, 1, 2, 0).reshape(C, C)

    def stacked_bias(b, roll=0):
        b = np.roll(b.reshape(4, 2, HC), roll, axis=2).transpose(1, 2, 0)
        return np.repeat(b[:, :, None, :], 2, axis=2).reshape(P)

    small = np.stack([stacked(a["L0_xattn_Wq"]), stacked(a["L0_xattn_Wq"], 4),
                      stacked(a["L0_xattn_Wk"]), stacked(a["L0_xattn_Wk"], 4),
                      a["L0_xattn_Wv"].T, a["L0_xattn_Wo"].T,
                      stacked(a["L1_xattn_Wq"]), stacked(a["L1_xattn_Wk"]), a["L1_xattn_Wv"].T], axis=1)
    bias = np.stack([stacked_bias(a["L0_xattn_bq"]), stacked_bias(a["L0_xattn_bq"], 4),
                     stacked_bias(a["L0_xattn_bk"]), stacked_bias(a["L0_xattn_bk"], 4),
                     np.tile(a["L0_xattn_bo"], 2),
                     stacked_bias(a["L1_xattn_bq"]), stacked_bias(a["L1_xattn_bk"])], axis=1)
    arrays = {
        "x": a["x"].reshape(TOKENS, T), "ctx": a["ctx_2048"].reshape(TOKENS, T),
        "small": small, "bias": bias,
        "bv0": np.tile(a["L0_xattn_bv"], (P, 4)), "bv1": np.tile(a["L1_xattn_bv"], (P, 4)),
        "wr0": a["L0_ffn_W_router"].reshape(2, P, E).transpose(1, 0, 2),
        "wr1": a["L1_ffn_router_weight"].reshape(2, P, E).transpose(1, 0, 2),
    }
    for L, (g, u, d) in enumerate((("L0_ffn_W_gate", "L0_ffn_W_up", "L0_ffn_W_down"),
                                   ("L1_ffn_gate_proj", "L1_ffn_up_proj", "L1_ffn_down_proj"))):
        w = np.concatenate([a[g], a[u]], axis=2).reshape(E, 2, P, 2 * I)
        arrays[f"gu{L}"] = w.transpose(2, 0, 1, 3)
        arrays[f"dn{L}"] = a[d].transpose(1, 0, 2)
    arrays["cos"], arrays["sin"] = rotary_tables()
    arrays = {f"in_{n}": np.ascontiguousarray(z) for n, z in arrays.items()}

    nc = bacc.Bacc("TRN2", target_bir_lowering=False, num_devices=1)
    ap = {n[3:]: nc.dram_tensor(n, z.shape, mybir.dt.from_np(z.dtype), kind="ExternalInput").ap()
          for n, z in arrays.items()}
    out = nc.dram_tensor("out", (TOKENS + P, T), F32, kind="ExternalOutput").ap()
    wts = dict(small=ap["small"], bias=ap["bias"], bv0=ap["bv0"], bv1=ap["bv1"], wr0=ap["wr0"], wr1=ap["wr1"],
               gu=(ap["gu0"], ap["gu1"]), dn=(ap["dn0"], ap["dn1"]))
    build(nc, ap["x"], ap["ctx"], (ap["cos"], ap["sin"]), wts, out)
    r = run_bass_kernel_spmd(nc, [arrays], core_ids=[0])
    return r.results[0]["out"][:TOKENS].reshape(B, C, T)
```

```python
from contextlib import ExitStack

import numpy as np

import concourse.bass as bass
from concourse import mybir

F32 = mybir.dt.float32
BF16 = mybir.dt.bfloat16
I32 = mybir.dt.int32
U32 = mybir.dt.uint32
ALU = mybir.AluOpType
ACT = mybir.ActivationFunctionType
AX = mybir.AxisListType

P = 128
B, C, T = 64, 64, 256
NH, HC = 8, 8
PAIRS = B // 2
TOKENS = B * C
E, I, K = 64, 96, 8
CAP = 2 * (512 * K) // E
TILES0 = TOKENS * K // P + E
UNITS = 16
GROUPS = 4
TERMS_Q = ((0, 3), (1, 2), (2, 1))
TERMS_K = ((0, 3), (0, 2), (0, 1))
MAXROW = 48
SCALE = float(HC) ** -0.5
EPS = 1e-5
MAGIC = 1597463007.0
LISTLEN = E * TOKENS
WIDTH = 2 * 2 * I + T
EARLY = 16

LAG = dict(load=0, comb=1, front=2, stack=3, smax=4, attn=5, back=6, route=7, place=8, post=9)
STEPS = PAIRS + LAG["post"]
LOOP0, LOOPN = 10, 7
PEELED = 6
FB = 8
NB = 3

MISC = {
    layer: [("RK", "place"), ("mT1", "attn"), ("K", "front"), ("V", "smax"), ("OT0", "back"), ("OT1", "back"),
            ("Q", "front"), ("NT", "back"), ("XT", "route"), ("mT0", "smax"), last, ("LG", "route")]
    for layer, last in enumerate((("WO", "back"), ("LIST", "place")))
}


class Step:

    def __init__(self, layer, s0, it=0):
        self.L, self.s0, self.it = layer, s0, it

    def on(self, stage):
        return 0 <= self.s0 - LAG[stage] < PAIRS

    def buf(self, stage):
        return (self.s0 - LAG[stage]) % NB

    def pair(self, stage):
        return self.s0 - LAG[stage] + self.it * 3

    def n(self, stage, per=1, extra=None):
        t0 = self.s0 - LAG[stage] + PAIRS * self.L
        extra = per if extra is None else extra
        return self.it * (3 * per) + (per * t0 + extra)

    def nbuf(self, stage, per=16):
        b = self.buf(stage)
        uses = len([t for t in range(PAIRS) if t % NB == b])
        t0 = self.s0 - LAG[stage]
        return self.it * per + per * (uses * self.L + t0 // NB + 1)

    def n1(self, stage, per=1, extra=None):
        extra = per if extra is None else extra
        return self.it * (3 * per) + (per * (self.s0 - LAG[stage]) + extra)

    def nbuf1(self, stage, per=16):
        return self.it * per + per * ((self.s0 - LAG[stage]) // NB + 1)

    def before(self, item):
        names = [name for name, _ in MISC[self.L]]
        i = names.index(item)
        bank, s = i % 2, self.s0
        while s >= 0:
            i -= 2
            if i < 0:
                i, s = i + len(names), s - 1
            if 0 <= s - LAG[MISC[self.L][i][1]] < PAIRS and s >= 0:
                return bank, MISC[self.L][i], Step(self.L, s, self.it)
        return bank, None, None


def steps(layer, engine, body):
    for s in range(LOOP0):
        body(Step(layer, s))
    with engine.Fori(0, LOOPN) as it:
        for c in range(NB):
            body(Step(layer, LOOP0 + c, it))
    for s in range(LOOP0 + NB * LOOPN, STEPS):
        body(Step(layer, s))


def row(t, n=P):
    return bass.ds(t * n, n)


def build(nc, x, ctx, tables, wts, out):
    stack = ExitStack()
    with stack:
        def sb(name, shape, dt=F32):
            return stack.enter_context(nc.sbuf_tensor(name, shape, dt))

        def sem(name):
            return stack.enter_context(nc.semaphore(name))

        def sems(name, n=NB):
            return [sem(f"{name}{i}") for i in range(n)]

        def dram(name, shape, dt=F32):
            return nc.dram_tensor(name, shape, dt).ap()

        stack_d = [dram(f"stack_d{b}", (2, 3, P, T), BF16) for b in range(NB)]
        x1_d = dram("x1_d", (TOKENS, T))
        x2_d = dram("x2_d", (TOKENS, T))
        xn_d = [dram("xn0_d", (TOKENS + P, T)), dram("xn1_d", (TOKENS + P, T + E))]
        list_d = dram("list_d", (LISTLEN, 1), I32)
        odd_d = dram("odd_d", (TOKENS + P, T))
        y0_d = dram("y0_d", (TILES0 * P, T))

        psS = [stack.enter_context(nc.psum_tensor(f"psS{i}", [P, 512], F32)) for i in range(3)]
        psE = [stack.enter_context(nc.psum_tensor(f"psE{i}", [P, 512], F32)) for i in range(2)]
        psO = stack.enter_context(nc.psum_tensor("psO", [P, 512], F32))
        psM = [stack.enter_context(nc.psum_tensor(f"psM{i}", [P, 512], F32)) for i in range(2)]

        ident = sb("ident", [P, P])
        ones = sb("ones", [P, P], BF16)
        tri = sb("tri", [P, P], BF16)
        iota_e = sb("iota_e", [P, E])
        iota_r = sb("iota_r", [P, P], BF16)
        iota_i = sb("iota_i", [P, P], I32)
        part1 = sb("part1", [P, 1])
        base0 = sb("base0", [P, E])
        one_row = sb("one_row", [P, T], BF16)
        total = sb("total", [P, E])
        id_acc = sb("id_acc", [P, E])
        tok0 = sb("tok0", [P, 1])

        part_i = sb("part_i", [P, 1], I32)
        slot_i = sb("slot_i", [P, 3], I32)
        base_i = sb("base_i", [P, E], I32)
        slotk = sb("slotk", [P, 3])
        top_all = sb("top_all", [P, PAIRS * K])
        place_all = sb("place_all", [P, PAIRS * K])
        row_all = sb("row_all", [P, PAIRS * K], I32)
        w_all = sb("w_all", [P, PAIRS * K])
        idx_e = sb("idx_e", [P, E], I32)

        wbd1 = {n: sb(f"proj_{n}1", [P, P]) for n in "qkv"}
        bias = sb("bias", [P, 9])
        wr = [sb(f"router{L}", [P, 2, E]) for L in range(2)]

        mv = sb("mv", [P, 2, 2])

        att = ExitStack()

        def ab(name, shape, dt=F32):
            return att.enter_context(nc.sbuf_tensor(name, shape, dt))

        cos = ab("cos", [P, T])
        sin = ab("sin", [P, T])
        wbd = [{n: ab(f"proj_{n}0", [P, P]) for n in "qrksvo"}, wbd1]
        wcmp = ab("wcmp", [P, 9, C])
        xin = [ab(f"xin{b}", [P, T]) for b in range(NB)]
        x2 = [ab(f"x2_{b}", [P, T]) for b in range(NB)]
        ctx_t = [ab(f"ctx{b}", [P, T]) for b in range(NB)]
        xres = [ab(f"xres{b}", [P, T]) for b in range(NB)]
        xn = [ab(f"xn{b}", [P, T]) for b in range(NB)]
        zrow = ab("zrow", [2, 8 * T], BF16)
        orow = ab("orow", [2, 8 * T], BF16)
        rope = ab("rope", [P, 2, 2, T])
        qk = [ab(f"qk{b}", [P, 2, T]) for b in range(NB)]
        rem = ab("rem", [P, 2, T])
        parts = [ab(f"parts{b}", [P, 2, 3, T], BF16) for b in range(NB)]
        q2 = [ab(f"q2_{b}", [P, 8, T], BF16) for b in range(NB)]
        k2 = [ab(f"k2_{b}", [P, 8, 2 * T], BF16) for b in range(NB)]
        mx = [ab(f"mx{b}", [P, 2, 16]) for b in range(NB)]
        mhi = [ab(f"mhi{h}", [P, 2, 8], BF16) for h in range(2)]
        msp = [ab(f"msp{h}", [P, 2, 2, 8]) for h in range(2)]
        mrow = [ab(f"mrow{h}", [32, P], BF16) for h in range(2)]
        v = [ab(f"v{b}", [P, 2, UNITS, 32]) for b in range(NB)]
        prob = [ab(f"prob{g}", [P, 4, 512]) for g in range(3)]
        osb = ab("osb", [P, GROUPS, T])
        rec = ab("rec", [P, 2, UNITS])
        nrm = ab("nrm", [P, 2, P])
        nt = ab("nt", [P, T])
        x1 = [ab(f"x1_{b}", [P, T]) for b in range(NB)]
        stats = ab("stats", [P, 2, 6])
        nwt = ab("nwt", [P, 6, 2])
        rstd = ab("rstd", [P, 2, 2])
        xr = [ab(f"xr{b}", [P, T + E]) for b in range(NB)]
        xT = ab("xT", [P, 2, P])
        logit = ab("logit", [P, E])
        rest = ab("rest", [P, E])
        top = [ab(f"top{b}", [P, 8]) for b in range(NB)]
        topi = [ab(f"topi{b}", [P, 8], U32) for b in range(NB)]
        topf = [ab(f"topf{b}", [P, 8]) for b in range(NB)]
        mask = [ab(f"mask{b}", [P, E], BF16) for b in range(NB)]
        ntop = ab("ntop", [P, 1])
        ex = ab("ex", [P, E])
        exm = ab("exm", [P, E])
        den = ab("den", [P, 2])
        place = ab("place", [P, E])
        eq = ab("eq", [P, K, E], BF16)
        hot = ab("hot", [P, K, E])
        posf = [ab(f"posf{b}", [P, K]) for b in range(NB)]
        posi = [ab(f"posi{b}", [P, K], I32) for b in range(NB)]
        toki = [ab(f"toki{b}", [P, 1], I32) for b in range(NB)]
        hotr = ab("hotr", [P, K, P], BF16)
        hote = ab("hote", [P, 2, K, E], BF16)
        posb = [ab(f"posb{b}", [P, K], I32) for b in range(NB)]
        yg = ab("yg", [P, K, T])
        zinit = prob[0][:, :, :].rearrange("p a b -> p (a b)").bitcast(I32)
        zf = xr[0]
        att.close()

        ffn = ExitStack()

        def fb(name, shape, dt=F32):
            return ffn.enter_context(nc.sbuf_tensor(name, shape, dt))

        xg = [fb(f"xg{b}", [P, T + E]) for b in range(FB)]
        idx = [fb(f"idx{b}", [P, 1], I32) for b in range(FB)]
        xgT = [fb(f"xgT{b}", [P, 2, P]) for b in range(2)]
        sil = [fb(f"sil{b}", [P, I]) for b in range(2)]
        hid = [fb(f"hid{b}", [P, I]) for b in range(2)]
        hT = [fb(f"hT{b}", [I, P]) for b in range(2)]
        y_all = fb("y_all", [P, FB, T])
        y = [y_all[:, b, :] for b in range(FB)]
        idx_s = [fb(f"idx_s{b}", [P, 1], I32) for b in range(FB)]
        wcol = [fb(f"wcol{b}", [P, 1]) for b in range(FB)]
        cnt = fb("cnt", [P, 6, E])
        cnti = fb("cnti", [P, E], I32)
        fhot = fb("fhot", [P, K, E])
        rowd = fb("rowd", [P, PAIRS * K])
        cumT = fb("cumT", [E, P])
        tri_f = fb("tri_f", [E, E])
        cmp_ = fb("cmp_", [P, 3, E])
        cmpm = fb("cmpm", [P, 3, E])
        owner = fb("owner", [P, 4, 3])
        tabrow = fb("tabrow", [1, 2, TILES0], I32)
        spare = (nc.sbuf_bytes_remaining - 4 * E * WIDTH) // 4
        if spare > 0:
            fb("spare", [P, spare])
        wt = fb("wt", [P, E, WIDTH])
        ffn.close()

        s_bar = sem("s_bar")
        s_pool_set, s_vec_set = sem("s_pool_set"), sem("s_vec_set")
        s_clear = sem("s_clear")
        d_small, d_setup, d_ones = sem("d_small"), sem("d_setup"), sem("d_ones")
        d_x, d_ctx, d_xres = sems("d_x"), sems("d_ctx"), sems("d_xres")
        d_parts, d_stack = sems("d_parts"), sems("d_stack")
        d_max = [sems("d_maxa"), sems("d_maxb")]
        d_x2, d_x1, d_xn, d_list = sems("d_x2"), sems("d_x1"), sems("d_xn"), sems("d_list")
        d_yg = sem("d_yg")
        s_comb = sem("s_comb")
        s_mvx, s_mvr, s_rstd = sem("s_mvx"), sem("s_mvr"), sem("s_rstd")
        s_xn, s_xr = sem("s_xn"), sem("s_xr")
        s_qp, s_kp, s_qr, s_kr, s_qk = (sem(n) for n in ("s_qp", "s_kp", "s_qr", "s_kr", "s_qk"))
        s_p1, s_rem, s_p2, s_p3 = (sem(n) for n in ("s_p1", "s_rem", "s_p2", "s_p3"))
        s_score, s_max = sem("s_score"), sem("s_max")
        s_msp, s_mT, s_mrow = sems("s_msp", 2), sems("s_mT", 2), sems("s_mrow", 2)
        s_st, s_exp = sem("s_st"), sem("s_exp")
        s_pv, s_oev = sem("s_pv"), sem("s_oev")
        s_vp, s_v = sem("s_vp"), sem("s_v")
        s_ot, s_nrm = sems("s_ot", 2), sems("s_nrm", 2)
        s_ntp, s_nt, s_wo, s_x1 = (sem(n) for n in ("s_ntp", "s_nt", "s_wo", "s_x1"))
        s_xtp, s_xT, s_lgp, s_logit = (sem(n) for n in ("s_xtp", "s_xT", "s_lgp", "s_logit"))
        s_top, s_topf, s_ntop, s_mask, s_rkp = (sem(n) for n in ("s_top", "s_topf", "s_ntop", "s_mask", "s_rkp"))
        s_place, s_tot, s_ex, s_wk, s_wall = (sem(n) for n in ("s_place", "s_tot", "s_ex", "s_wk", "s_wall"))
        s_hot, s_posf, s_posi, s_lhs, s_lsp, s_list = (
            sem(n) for n in ("s_hot", "s_posf", "s_posi", "s_lhs", "s_lsp", "s_list"))
        s_eq, s_hote = sem("s_eq"), sem("s_hote")
        s_posb, s_fhot, s_row = sem("s_posb"), sem("s_fhot"), sem("s_row")
        s_chain = sem("s_chain")
        s_held = sem("s_held")
        d_w = sems("d_w", E // FB)
        s_r1, s_r2, s_r3 = sem("s_r1"), sem("s_r2"), sem("s_r3")
        d_idx, d_xg, d_y = sems("d_idx", FB), sems("d_xg", FB), sems("d_y", FB)
        s_idx, s_xp, s_xgT, s_gup, s_sil, s_hid, s_hp, s_hT, s_yp, s_y, s_wcol = (
            sem(n) for n in ("s_idx", "s_xp", "s_xgT", "s_gup", "s_sil", "s_hid", "s_hp", "s_hT",
                             "s_yp", "s_y", "s_wcol"))
        d_acc = sems("d_acc", 2)
        d_zero, d_sum = sem("d_zero"), sem("d_sum")

        block = stack.enter_context(nc.Block())

        def barrier(eng, k):
            eng.drain().then_inc(s_bar, 1)
            eng.wait_ge(s_bar, 5 * k)

        def wait(eng, semaphore, value):
            if not isinstance(value, int) or value > 0:
                eng.wait_ge(semaphore, value)

        def hold(eng, semaphore, value):
            wait(eng, semaphore, value)
            if not isinstance(value, int):
                eng.sem_inc(s_held, 1)

        def uses_of(b):
            return len([t for t in range(PAIRS) if t % NB == b])

        def last(st, stage, per=1, back=1):
            return st.n(stage, per, per * (1 - back))

        def lastbuf(st, stage, per=16):
            return st.nbuf(stage, per) - per

        FREE = dict(mT0=s_mrow[0], mT1=s_mrow[1], V=s_v, OT0=s_nrm[0], OT1=s_nrm[1], Q=s_qr, K=s_kr,
                    NT=s_nt, WO=s_x1, XT=s_xT, LG=s_logit, RK=s_tot, LIST=s_list)

        def bank(pe, st, item):
            at, before, then = st.before(item)
            if before:
                name, stage = before
                if name == "LIST":
                    pe.wait_ge(s_list, then.n1(stage))
                elif name == "NT" and st.L == 1:
                    pe.wait_ge(s_x1, then.n(stage))
                else:
                    pe.wait_ge(FREE[name], then.n(stage))
            return psM[at]

        def over_k(tile):
            return tile[:, :].unsqueeze(1).broadcast_to((P, K, tile.shape[1]))

        def over_e(tile, n=E):
            return tile[:, :].unsqueeze(2).broadcast_to((P, K, n))

        def head_cols(tile, o, n):
            return tile[:, :].rearrange("p (h r) -> p h r", r=32)[:, :, o:o + n]

        def item_bank(L, name):
            return [n for n, _ in MISC[L]].index(name) % 2

        FLAG = dict(idx=0, gather=4, X=8, GU=9, H=10, D=11)
        JOBS = (TILES0, E)

        class Slot:

            def __init__(self, layer, s0, it=0):
                self.L, self.s0, self.it = layer, s0, it

            def on(self, stage):
                return 0 <= self.s0 - FLAG[stage] < JOBS[self.L]

            def job(self, stage):
                return self.s0 - FLAG[stage] + self.it * FB

            def pair_job(self, stage):
                return (self.s0 - FLAG[stage]) // 2 + self.it * (FB // 2)

            def buf(self, stage, n=FB):
                return (self.s0 - FLAG[stage]) % n

            def n(self, stage, back=0):
                return self.it * FB + (self.s0 - FLAG[stage] + 1 - back + (JOBS[0] if self.L else 0))

            def nbuf(self, stage, back=0):
                return self.it * 16 + 16 * ((self.s0 - FLAG[stage]) // FB + 1 - back
                                            + (JOBS[0] // FB if self.L else 0))

            def nbuf0(self, stage, back=0):
                return self.it * 16 + 16 * ((self.s0 - FLAG[stage]) // FB + 1 - back)

        def slots(layer, eng, body, look_up=None, before=None, aside=None):
            def group(first, n, it=0, beside=True):
                table = look_up(Slot(layer, first, it)) if look_up else None
                for c in range(n):
                    body(Slot(layer, first + c, it), table)
                    if aside and beside:
                        aside(it + first // FB, c)

            for g in range(PEELED):
                if before:
                    before(g)
                group(g * FB, FB)
            if before:
                before(PEELED)
            start, count = PEELED, JOBS[layer] // FB - PEELED
            if aside:
                with eng.Fori(0, PAIRS - PEELED) as it:
                    group(start * FB, FB, it)
                start, count = PAIRS, count - (PAIRS - PEELED)
            with eng.Fori(0, count) as it:
                group(start * FB, FB, it, False)
            end = JOBS[layer] + FLAG["D"]
            for s in range(JOBS[layer], end, FB):
                group(s, min(FB, end - s), 0, False)

        def look_up(engine, column, first_stage, last_stage):
            def read(st):
                lo, hi = st.s0 - FLAG[first_stage], st.s0 + FB - 1 - FLAG[last_stage]
                if isinstance(st.it, int):
                    lo, hi = max(lo, 0), min(hi, TILES0 - 1)
                if hi < lo:
                    return {}
                most = (LISTLEN - P, E - 1)[column]
                _, values = nc.values_load_multi_w_load_instructions(
                    tabrow[0:1, column, bass.ds(lo + st.it * FB, hi - lo + 1)], engines=(engine,),
                    min_val=0, max_val=most, skip_runtime_bounds_check_because="the table is clamped")
                return {lo + i: value for i, value in enumerate(values)}
            return read

        def load_weights(eng, layer, e):
            at = E - 1 - e
            eng.dma_start(wt[:, at, 0:4 * I], wts["gu"][layer][:, e, :]).then_inc(d_w[e // FB], 16)
            eng.dma_start(wt[0:I, at, 4 * I:WIDTH], wts["dn"][layer][:, e, :]).then_inc(d_w[e // FB], 16)

        def sp_slot(st, first_row):
            sp = nc.sync
            if st.on("idx"):
                b = st.buf("idx")
                hold(sp, d_xg[b], st.nbuf0("idx", 1))
                sp.dma_start(idx[b][:, :], list_d[bass.ds(first_row[st.s0 - FLAG["idx"]], P), :])\
                  .then_inc(d_idx[b], 16)
            if st.on("D"):
                b = st.buf("D")
                hold(sp, s_y, st.n("D"))
                sp.dma_start(y0_d[row(st.job("D")), :], y[b]).then_inc(d_y[b], 16)

        @block.sync
        def _(sp):
            loads = [(cos[:, :], tables[0]), (sin[:, :], tables[1]), (bias[:, :], wts["bias"]),
                     (wr[0][:, :, :], wts["wr0"]), (wr[1][:, :, :], wts["wr1"]),
                     (wcmp[0:C, :, :], wts["small"]), (wcmp[C:P, :, :], wts["small"])]
            for dst, src in loads:
                sp.dma_start(dst, src).then_inc(d_small, 16)
            def ones_rows(L):
                sp.wait_ge(s_clear, 2 * L + 1)
                for b in range(NB):
                    for hh in range(2):
                        sp.dma_start(k2[b][64 * hh + MAXROW:64 * hh + MAXROW + 2, :, hh * T:(hh + 1) * T],
                                     orow[:, :].rearrange("p (g t) -> p g t", t=T)).then_inc(d_ones, 16)
                sp.wait_ge(d_ones, 16 * 2 * NB * (L + 1))

            sp.wait_ge(s_pool_set, 1)
            sp.dma_start(list_d.rearrange("(p n) o -> p (n o)", p=P), zinit[:, :]).then_inc(d_setup, 16)
            sp.dma_start(xn_d[0][TOKENS:TOKENS + P, :], zf[:, 0:T]).then_inc(d_setup, 16)
            sp.dma_start(xn_d[1][TOKENS:TOKENS + P, :], zf[:, :]).then_inc(d_setup, 16)
            sp.dma_start(out[TOKENS:TOKENS + P, :], zf[:, 0:T]).then_inc(d_setup, 16)
            ones_rows(0)
            sp.wait_ge(d_setup, 16 * 4)
            barrier(sp, 1)

            def body(st):
                L = st.L
                if st.on("load"):
                    b, t = st.buf("load"), st.pair("load")
                    hold(sp, s_xn, last(st, "load", back=NB))
                    sp.dma_start(xin[b][:, :], (x, x1_d)[L][row(t), :]).then_inc(d_x[b], 16)
                if st.on("attn"):
                    b, t = st.buf("attn"), st.pair("attn")
                    hold(sp, s_x1, last(st, "attn", back=NB))
                    if L == 1:
                        hold(sp, d_x2[b], st.nbuf1("attn"))
                    sp.dma_start(xres[b][:, :], (x, x2_d)[L][row(t), :]).then_inc(d_xres[b], 16)
                if st.on("post") and L == 1:
                    b, t = st.buf("post"), st.pair("post")
                    hold(sp, s_wall, st.n1("post"))
                    sp.dma_start(xn_d[1][row(t), :], xr[b][:, :]).then_inc(d_xn[b], 16)
                if st.on("attn"):
                    b = st.buf("attn")
                    hold(sp, s_mrow[1], st.n("attn"))
                    for hh in range(2):
                        sp.dma_start(q2[b][64 * hh + MAXROW:64 * hh + MAXROW + 2, 4:8, :].rearrange("p g t -> p (g t)"),
                                     mrow[1][16 * hh:16 * hh + 16, :]).then_inc(d_max[1][b], 16)
                if st.on("stack"):
                    b = st.buf("stack")
                    hold(sp, s_p3, st.n("stack"))
                    hold(sp, d_stack[b], lastbuf(st, "stack", 16 * 14))
                    sp.dma_start(stack_d[b].rearrange("q a p t -> p (q a) t"),
                                 parts[b][:, :, :, :].rearrange("p q a t -> p (q a) t")).then_inc(d_parts[b], 16)
                if st.on("comb"):
                    b, t = st.buf("comb"), st.pair("comb")
                    hold(sp, s_vp, last(st, "comb", back=NB))
                    sp.dma_start(ctx_t[b][:, :], ctx[row(t), :]).then_inc(d_ctx[b], 16)
                if st.on("stack"):
                    b = st.buf("stack")
                    hold(sp, s_st, last(st, "stack", UNITS, back=NB))
                    hold(sp, d_parts[b], st.nbuf("stack"))
                    for hh in range(2):
                        r = 64 * hh
                        for (part, n), (kpart, kn) in zip(TERMS_Q, TERMS_K):
                            src = stack_d[b][0, part, 64 * hh:64 * hh + 64, :]
                            sp.dma_start(q2[b][r:r + 8 * n, :, :],
                                         bass.AP(src.tensor, src.offset, [[0, n], [8 * T, 8], [T, 8], [1, T]]))\
                              .then_inc(d_stack[b], 16)
                            src = stack_d[b][1, kpart, 64 * hh:64 * hh + 64, :]
                            sp.dma_start(k2[b][r:r + 8 * n, :, hh * T:(hh + 1) * T],
                                         bass.AP(src.tensor, src.offset, [[P * T, n], [8 * T, 8], [T, 8], [1, T]]))\
                              .then_inc(d_stack[b], 16)
                            r += 8 * n
                        sp.dma_start(q2[b][r:r + 2, :, :].rearrange("p g t -> p (g t)"), zrow[:, :])\
                          .then_inc(d_stack[b], 16)
                if st.on("route") and L == 0:
                    b, t = st.buf("route"), st.pair("route")
                    hold(sp, s_xr, st.n("route"))
                    sp.dma_start(xn_d[0][row(t), :], xr[b][:, 0:T]).then_inc(d_xn[b], 16)
                if st.on("comb") and L == 1:
                    b, t = st.buf("comb"), st.pair("comb")
                    hold(sp, s_comb, st.n1("comb", K))
                    sp.dma_start(x2_d[row(t), :], x2[b][:, :]).then_inc(d_x2[b], 16)
                if st.on("smax"):
                    b = st.buf("smax")
                    hold(sp, s_mrow[0], st.n("smax"))
                    for hh in range(2):
                        sp.dma_start(q2[b][64 * hh + MAXROW:64 * hh + MAXROW + 2, 0:4, :].rearrange("p g t -> p (g t)"),
                                     mrow[0][16 * hh:16 * hh + 16, :]).then_inc(d_max[0][b], 16)
                if st.on("back"):
                    b, t = st.buf("back"), st.pair("back")
                    hold(sp, s_x1, st.n("back"))
                    sp.dma_start((x1_d, out)[L][row(t), :], x1[b][:, :]).then_inc(d_x1[b], 16)

            for L in range(2):
                if L == 1:
                    zeros = xn_d[1][TOKENS:TOKENS + P, 0:T]
                    sp.dma_start(odd_d.rearrange("(n p) t -> n p t", p=P),
                                 zeros.unsqueeze(0).broadcast_to((PAIRS + 1, P, T))).then_inc(d_zero, 16)
                    ones_rows(1)
                    barrier(sp, 4)
                steps(L, sp, body)
                for b in range(NB):
                    sp.wait_ge(d_x1[b], 16 * (L + 1) * uses_of(b))
                    sp.wait_ge(d_xn[b], 16 * (L + 1) * uses_of(b))
                barrier(sp, 2 + 3 * L)
                if L == 0:
                    sp.wait_ge(s_r3, 2)
                    slots(L, sp, sp_slot, look_up(mybir.EngineType.SP, 0, "idx", "idx"))
                    for b in range(FB):
                        sp.wait_ge(d_y[b], 16 * TILES0 // FB)
                barrier(sp, 3 + 3 * L)

        @block.gpsimd
        def _(pool):
            g = nc.gpsimd

            def clear():
                g.memset(zrow[:, :], 0.0)
                for b in range(NB):
                    g.memset(q2[b][:, :, :], 0.0)

            g.memset(ident[:, :], 0.0)
            g.memset(zf[:, :], 0.0)
            g.memset(one_row[:, :], 1.0)
            g.memset(zinit[:, :], TOKENS)
            g.iota(iota_i[:, :], [[1, P]], base=0, channel_multiplier=0)
            pool.drain().then_inc(s_pool_set, 1)
            pool.wait_ge(s_pool_set, 1)
            g.affine_select(out=ident[:, :], in_=ident[:, :], compare_op=ALU.not_equal, fill=1.0,
                            base=0, pattern=[[-1, P]], channel_multiplier=1)
            g.affine_select(out=tri[:, :], in_=one_row[:, 0:P], compare_op=ALU.is_gt, fill=0.0,
                            base=0, pattern=[[1, P]], channel_multiplier=-1)
            g.iota(part_i[:, 0:1], [[0, 1]], base=0, channel_multiplier=1)
            g.iota(slot_i[:, :], [[P, 3]], base=0, channel_multiplier=1)
            g.iota(base_i[:, :], [[TOKENS, E]], base=0, channel_multiplier=0)
            pool.drain().then_inc(s_pool_set, 1)
            clear()
            barrier(pool, 1)

            def body(st):
                L = st.L
                if st.on("place"):
                    b = st.buf("place")
                    hit = eq[:, :, :] if L == 0 else hote[:, 0, :, :]
                    hold(pool, s_eq, st.n("place"))
                    hold(pool, s_place, st.n("place"))
                    hold(pool, s_posf, last(st, "place"))
                    g.tensor_tensor(hot[:, :, :], hit, over_k(place), ALU.mult).then_inc(s_hot, 1)
                    if L == 1:
                        g.tensor_scalar(hote[:, 1, :, :], hit, part1[:, 0:1], None, ALU.mult).then_inc(s_hote, 1)
                if L == 1 and st.on("load"):
                    b = st.buf("load")
                    hold(pool, s_posb, st.n1("load"))
                    for k in range(K):
                        if st.s0 > LAG["load"]:
                            hold(pool, s_comb, st.n1("load", K, k + 1 - K))
                        g.indirect_dma_start(yg[:, k, :], None, y0_d[:, :],
                                             bass.IndirectOffsetOnAxis(posb[b][:, k:k + 1], 0)).then_inc(d_yg, 16)
                if L == 0 and st.on("post"):
                    b = st.buf("post")
                    hold(pool, s_posi, st.n1("post"))
                    for k in range(K):
                        g.indirect_dma_start(list_d[:, :], bass.IndirectOffsetOnAxis(posi[b][:, k:k + 1], 0),
                                             toki[b][:, 0:1], None).then_inc(d_list[b], 16)
                if st.on("front"):
                    b = st.buf("front")
                    if L == 0:
                        hold(pool, s_qr, st.n("front"))
                        hold(pool, s_kr, st.n("front"))
                        g.tensor_tensor(qk[b][:, :, :], rope[:, 0, :, :], rope[:, 1, :, :], ALU.add).then_inc(s_qk, 1)
                        hold(pool, s_qk, st.n("front"))
                    hold(pool, s_p1, st.n("front"))
                    if L == 1:
                        hold(pool, s_qr, st.n("front"))
                    hold(pool, s_p3, last(st, "front"))
                    g.tensor_tensor(rem[:, :, :], qk[b][:, :, :], parts[b][:, :, 0, :], ALU.subtract).then_inc(s_rem, 1)
                    hold(pool, s_p2, st.n("front"))
                    hold(pool, s_rem, st.n("front"))
                    g.tensor_tensor(parts[b][:, :, 2, :], rem[:, :, :], parts[b][:, :, 1, :], ALU.subtract).then_inc(s_p3, 1)

            def slot_body(st, table):
                L = st.L
                if st.on("gather"):
                    b = st.buf("gather")
                    if L == 0:
                        hold(pool, d_idx[b], st.nbuf0("gather"))
                    else:
                        hold(pool, s_idx, st.n("gather") - JOBS[0])
                    hold(pool, s_xp, st.n("gather", FB))
                    if L == 1:
                        hold(pool, s_wcol, st.n("gather", FB) - JOBS[0])
                    g.indirect_dma_start(xg[b][:, 0:(T, T + E)[L]], None, xn_d[L][:, :],
                                         bass.IndirectOffsetOnAxis(idx[b][:, 0:1], 0)).then_inc(d_xg[b], 16)
                if st.on("D") and L == 1:
                    b = st.buf("D")
                    hold(pool, s_y, st.n("D"))
                    odd = st.buf("D", 2)
                    hold(pool, d_acc[odd], st.pair_job("D") * 16)
                    g.indirect_dma_start((out, odd_d)[odd][:, :], bass.IndirectOffsetOnAxis(idx_s[b][:, 0:1], 0),
                                         y[b], None, compute_op=ALU.add).then_inc(d_acc[odd], 16)

            for L in range(2):
                if L == 1:
                    clear()
                    barrier(pool, 4)
                steps(L, pool, body)
                if L == 0:
                    for b in range(NB):
                        pool.wait_ge(d_list[b], 16 * K * uses_of(b))
                barrier(pool, 2 + 3 * L)
                if L == 1:
                    pool.wait_ge(d_zero, 16)
                    pool.wait_ge(s_r2, 4)
                slots(L, pool, slot_body)
                if L == 1:
                    for odd in range(2):
                        pool.wait_ge(d_acc[odd], 16 * E // 2)
                    g.dma_start(out[0:TOKENS, :], odd_d[0:TOKENS, :], accum_op=ALU.add,
                                max_dma_last_dim=4096).then_inc(d_sum, 16)
                    pool.wait_ge(d_sum, 16)
                barrier(pool, 3 + 3 * L)

        @block.scalar
        def _(act):
            a = nc.scalar
            barrier(act, 1)

            def body(st):
                L = st.L

                def o_out(stage, q):
                    if not st.on(stage):
                        return
                    act.wait_ge(s_pv, st.n(stage, 4, q + 1))
                    if q == 0:
                        wait(act, s_ot[1], last(st, stage))
                    a.copy(osb[:, q, :], psO[:, (q % 2) * T:(q % 2 + 1) * T]).then_inc(s_oev, 1)

                def max_rows(stage, h):
                    act.wait_ge(s_mT[h], st.n(stage))
                    wait(act, d_max[h][(st.s0 - LAG[stage] - 1) % NB], Step(L, st.s0 - 1, st.it).nbuf(stage, 32)
                         if st.s0 - 1 >= LAG[stage] else 0)
                    a.copy(mrow[h][:, :], psM[item_bank(L, f"mT{h}")][0:32, 0:P]).then_inc(s_mrow[h], 1)

                for u in range(UNITS):
                    if u == 15 and st.s0 < EARLY // 2:
                        for e in (2 * st.s0, 2 * st.s0 + 1):
                            load_weights(act, L, e)
                    if st.on("attn"):
                        act.wait_ge(s_st, st.n("attn", UNITS, u + 1))
                        if u % 4 == 0:
                            wait(act, s_pv, st.n("attn", 4, u // 4 - 2))
                        gr = (4 * (st.s0 - LAG["attn"]) + u // 4) % 3
                        ring = u % 2
                        a.activation(prob[gr][:, u % 4, :], psE[ring][:, :], ACT.Exp, scale=SCALE).then_inc(s_exp, 1)
                    if u == 0:
                        o_out("back", 2)
                    if u == 4:
                        o_out("back", 3)
                    if u == 8:
                        o_out("attn", 0)
                    if u == 12:
                        o_out("attn", 1)
                    if u == 1 and st.on("attn"):
                        max_rows("attn", 1)
                    if u == 12 and st.on("smax"):
                        max_rows("smax", 0)
                    if u == 6 and (st.on("front") or st.on("route")):
                        act.wait_ge(s_rstd, st.it * 3 + (st.s0 - 1 + L * (STEPS - 4)))
                    if u == 6 and st.on("front"):
                        b = st.buf("front")
                        wait(act, s_qp, last(st, "front", back=NB))
                        a.activation(xn[b][:, :], (xin, x2)[L][b][:, :], ACT.Identity, bias=rstd[:, 1, 0:1],
                                     scale=rstd[:, 0, 0:1]).then_inc(s_xn, 1)
                    if u == 6 and st.on("route"):
                        b = st.buf("route")
                        wait(act, d_xn[b], lastbuf(st, "route"))
                        a.activation(xr[b][:, 0:T], x1[b][:, :], ACT.Identity, bias=rstd[:, 1, 1:2],
                                     scale=rstd[:, 0, 1:2]).then_inc(s_xr, 1)
                    if u == 4 and st.on("smax"):
                        b = st.buf("smax")
                        act.wait_ge(s_vp, st.n("smax"))
                        wait(act, s_pv, last(st, "smax", 4, back=NB))
                        a.copy(v[b][:, :, :, 0:HC],
                               psM[item_bank(L, "V")][:, 0:2 * P].rearrange("p (s h c) -> p s h c", s=2, c=HC))\
                         .then_inc(s_v, 1)
                    if u == 11 and st.on("front"):
                        b = st.buf("front")
                        act.wait_ge(s_qk if L == 0 else s_qr, st.n("front"))
                        wait(act, d_parts[b], lastbuf(st, "front"))
                        a.copy(parts[b][:, :, 0, :], qk[b][:, :, :]).then_inc(s_p1, 1)
                    if u == 13 and st.on("front"):
                        b = st.buf("front")
                        act.wait_ge(s_rem, st.n("front"))
                        a.copy(parts[b][:, :, 1, :], rem[:, :, :]).then_inc(s_p2, 1)
                    if u == 1 and st.on("place"):
                        b = st.buf("place")
                        act.wait_ge(s_ntop, st.n("place"))
                        wait(act, s_wk if L == 0 else s_wall, st.n1("place", 1, 0))
                        if L == 0:
                            a.activation(ex[:, 0:K], top[b][:, :], ACT.Exp, bias=ntop[:, 0:1]).then_inc(s_ex, 1)
                        else:
                            a.activation(ex[:, :], logit[:, :], ACT.Exp, bias=ntop[:, 0:1]).then_inc(s_ex, 1)
                    if L == 1 and u in (8, 4) and st.on("front"):
                        b, i = st.buf("front"), (8, 4).index(u)
                        act.wait_ge((s_qp, s_kp)[i], st.n("front"))
                        wait(act, s_rem, last(st, "front", back=NB))
                        a.activation(qk[b][:, i, :], psM[item_bank(1, "QK"[i])][:, 0:T], ACT.Identity,
                                     bias=bias[:, 5 + i:6 + i]).then_inc((s_qr, s_kr)[i], 1)
                    if L == 0 and u == 9 and st.on("back"):
                        act.wait_ge(s_ntp, st.n("back"))
                        wait(act, s_wo, last(st, "back"))
                        a.activation(nt[:, :], psM[item_bank(0, "NT")][:, 0:T], ACT.Identity,
                                     bias=bias[:, 7:8]).then_inc(s_nt, 1)
                    if u == 11 and st.on("route"):
                        act.wait_ge(s_xtp, st.n("route"))
                        wait(act, s_lgp, last(st, "route"))
                        a.copy(xT[:, :, :].rearrange("p c t -> p (c t)"), psM[item_bank(L, "XT")][:, 0:2 * P]).then_inc(s_xT, 1)
                    if u == 13 and st.on("route"):
                        act.wait_ge(s_lgp, st.n("route"))
                        wait(act, s_mask, last(st, "route"))
                        wait(act, s_ex, last(st, "route"))
                        a.copy(logit[:, :], psM[item_bank(L, "LG")][:, 0:E]).then_inc(s_logit, 1)

            def slot_body(st, table):
                if isinstance(st.it, int) and st.s0 < E - EARLY:
                    load_weights(act, st.L, st.s0 + EARLY)
                if st.on("X"):
                    act.wait_ge(s_xp, st.n("X"))
                    wait(act, s_gup, st.n("X", 2))
                    a.copy(xgT[st.buf("X", 2)][:, :, :].rearrange("p c t -> p (c t)"),
                           psS[st.buf("X", 2)][:, 0:2 * P]).then_inc(s_xgT, 1)
                if st.on("GU"):
                    act.wait_ge(s_gup, st.n("GU"))
                    wait(act, s_hid, st.n("GU", 2))
                    a.activation(sil[st.buf("GU", 2)][:, :], psE[st.buf("GU", 2)][:, 0:I], ACT.Silu).then_inc(s_sil, 1)
                if st.on("D") and st.L == 0:
                    act.wait_ge(s_yp, st.n("D"))
                    wait(act, d_y[st.buf("D")], st.nbuf0("D", 1))
                    a.copy(y[st.buf("D")], psM[st.buf("D", 2)][:, 0:T]).then_inc(s_y, 1)

            for L in range(2):
                if L == 1:
                    barrier(act, 4)
                steps(L, act, body)
                barrier(act, 2 + 3 * L)
                slots(L, act, slot_body)
                barrier(act, 3 + 3 * L)

        @block.vector
        def _(dve):
            v_ = nc.vector

            class Chain:
                n, it, per = 0, 0, 0

                marks = {}

                def add(self, ins, name=None):
                    ins.then_inc(s_chain, 1)
                    self.n += 1
                    self.marks[name] = self.n

                def join(self, name=None):
                    n = self.marks[name] if name else self.n
                    if isinstance(self.it, int):
                        dve.wait_ge(s_chain, n)
                    else:
                        hold(dve, s_chain, self.it * self.per + n)

            ch = Chain()

            def clear(L):
                v_.memset(orow[:, :], 1.0)
                for b in range(NB):
                    v_.memset(k2[b][:, :, :], 0.0)
                dve.drain().then_inc(s_clear, 1)
                for b in range(NB):
                    v_.memset(v[b][:, :, :, :], 0.0)
                dve.drain().then_inc(s_clear, 1)
                dve.wait_ge(s_clear, 2 * L + 2)
                for b in range(NB):
                    v_.memset(v[b][:, :, :, 8:9], 1.0)

            clear(0)
            v_.memset(mv[:, :, :], 1.0)
            v_.memset(ones[:, :], 1.0)
            v_.memset(id_acc[:, :], 0.0)
            v_.memset(tok0[:, :], 0.0)
            for w in wbd:
                for tile in w.values():
                    v_.memset(tile[:, :], 0.0)
            dve.drain().then_inc(s_vec_set, 1)
            dve.wait_ge(s_vec_set, 1)
            dve.wait_ge(s_pool_set, 2)
            v_.tensor_copy(iota_e[:, :], iota_i[:, 0:E])
            v_.tensor_copy(iota_r[:, :], iota_i[:, :])
            for b in range(NB):
                v_.tensor_scalar(toki[b][:, :], part_i[:, :], float((b - NB) * P), None, ALU.add)
            v_.tensor_copy(slotk[:, :], slot_i[:, :])
            v_.tensor_copy(base0[:, :], base_i[:, :])
            v_.tensor_copy(total[:, :], base_i[:, :])
            v_.tensor_scalar(part1[:, :], part_i[:, :], 1.0, None, ALU.add)
            dve.drain().then_inc(s_vec_set, 2)
            dve.wait_ge(d_small, 16 * 7)
            place_of = [(0, n) for n in "qrksvo"] + [(1, n) for n in "qkv"]
            for i, (L, n) in enumerate(place_of):
                for b in range(2):
                    rows = slice(C * b, C * b + C)
                    if n in "vo":
                        dst, src = wbd[L][n][rows, C * b:C * b + C], wcmp[rows, i, :]
                    else:
                        dst = wbd[L][n][rows, :].rearrange("p (r b g) -> p r b g", b=2, g=4)[:, :, b, :]
                        src = wcmp[rows, i, :].rearrange("p (r g) -> p r g", g=4)
                    v_.tensor_copy(dst, src)
            barrier(dve, 1)

            def newton(i):
                ve, y0, t1, t2 = nwt[:, 0, :], nwt[:, 1, :], nwt[:, 2, :], nwt[:, 3, :]
                if i:
                    ch.join("newton")
                if i == 0:
                    ins = v_.tensor_scalar(ve, mv[:, :, 1], EPS, None, ALU.add)
                elif i == 1:
                    ins = v_.tensor_scalar(y0.bitcast(I32), ve.bitcast(I32), -0.5, MAGIC, ALU.mult, ALU.add)
                elif i % 3 == 2:
                    ins = v_.tensor_tensor(t1, ve, y0, ALU.mult)
                elif i % 3 == 0:
                    ins = v_.scalar_tensor_tensor(t2, t1, -0.5, y0, ALU.mult, ALU.mult)
                elif i < 10:
                    ins = v_.scalar_tensor_tensor(y0, t2, 1.5, y0, ALU.add, ALU.mult)
                else:
                    ins = v_.scalar_tensor_tensor(rstd[:, 0, :], t2, 1.5, y0, ALU.add, ALU.mult)
                ch.add(ins, "newton")

            def body(st):
                L, it = st.L, st.it

                def red(u):
                    b = st.buf("smax")
                    bg, tt = u // 2, u % 2
                    dve.wait_ge(s_score, st.n("smax", UNITS, u + 1))
                    v_.tensor_reduce(mx[b][:, bg // 4, :].rearrange("p (h r) -> p h r", h=2)[:, :, (bg % 4) * 2 + tt],
                                     psS[(UNITS * (st.s0 - LAG["smax"]) + u) % 3][:, :].rearrange("p (h s) -> p h s", h=2), AX.X, ALU.max)\
                      .then_inc(s_max, 1)

                def negate_max(h):
                    b = st.buf("smax")
                    m = mx[b][:, h, :].rearrange("p (h r) -> p h r", h=2)
                    dve.wait_ge(s_max, st.n("smax", UNITS, 8 * h + 8))
                    ch.add(v_.tensor_scalar(mhi[h][:, :, :], m, -1.0, None, ALU.mult), "max")

                def split_max(h):
                    b = st.buf("smax")
                    m = mx[b][:, h, :].rearrange("p (h r) -> p h r", h=2)
                    wait(dve, s_mT[h], last(st, "smax"))
                    ch.join("max")
                    v_.tensor_copy(msp[h][:, :, 0, :], mhi[h][:, :, :]).then_inc(s_msp[h], 1)
                    v_.scalar_tensor_tensor(msp[h][:, :, 1, :], m, -1.0, mhi[h][:, :, :], ALU.mult, ALU.subtract)\
                      .then_inc(s_msp[h], 1)

                def invert(h):
                    ps = psM[item_bank(L, f"OT{h}")]
                    dve.wait_ge(s_ot[h], st.n("back"))
                    ch.add(v_.reciprocal(rec[:, h, :], head_cols(ps, 8, 1).rearrange("p h o -> p (h o)")), f"rec{h}")

                def normalise(h):
                    ps = psM[item_bank(L, f"OT{h}")]
                    wait(dve, s_ntp, last(st, "back"))
                    ch.join(f"rec{h}")
                    r = rec[:, h, :]
                    v_.tensor_tensor(nrm[:, h, :].rearrange("p (h c) -> p h c", c=HC), head_cols(ps, 0, HC),
                                     bass.AP(r.tensor, r.offset, [list(r.ap[0]), [1, UNITS], [0, HC]]),
                                     ALU.mult).then_inc(s_nrm[h], 1)

                def rotate(i):
                    b = st.buf("front")
                    ps = psM[item_bank(0, "QK"[i])]
                    dve.wait_ge((s_qp, s_kp)[i], st.n("front"))
                    wait(dve, s_qk, last(st, "front"))
                    v_.scalar_tensor_tensor(rope[:, 0, i, :], ps[:, 0:T], bias[:, 2 * i:2 * i + 1], cos[:, :],
                                            ALU.add, ALU.mult)
                    v_.scalar_tensor_tensor(rope[:, 1, i, :], ps[:, T:2 * T], bias[:, 2 * i + 1:2 * i + 2], sin[:, :],
                                            ALU.add, ALU.mult).then_inc((s_qr, s_kr)[i], 1)

                for u in range(UNITS):
                    if st.on("smax"):
                        red(u)
                    norms = st.on("front") or st.on("route")
                    if u == 0:
                        if st.on("front"):
                            dve.wait_ge(s_mvx, st.n("front"))
                        if st.on("route"):
                            dve.wait_ge(s_mvr, st.n("route"))
                    if u <= 5 and norms:
                        newton(2 * u)
                    if u == 0 and L == 1 and st.on("load"):
                        hold(dve, d_yg, st.n1("load", 16 * K, 0) - 32 * K)
                        v_.tensor_copy(posb[st.buf("load")][:, :], row_all[:, row(st.pair("load"), K)])\
                          .then_inc(s_posb, 1)
                    if u == 1 and st.on("place"):
                        dve.wait_ge(s_rkp, st.n("place"))
                        wait(dve, s_tot, st.n("place", 1, 0))
                        wait(dve, s_hot, last(st, "place"))
                        v_.tensor_tensor(place[:, :], psM[item_bank(L, "RK")][:, 0:E], total[:, :], ALU.add)\
                          .then_inc(s_place, 1)
                        dve.wait_ge(s_place, st.n("place"))
                        v_.tensor_tensor(total[:, :], psM[item_bank(L, "RK")][:, E:2 * E], total[:, :], ALU.add)\
                          .then_inc(s_tot, 1)
                    if u == 0 and st.on("place"):
                        b = st.buf("place")
                        dve.wait_ge(s_topf, st.n("place"))
                        if L == 1:
                            wait(dve, s_hote, st.n1("place", 1, 0))
                            wait(dve, s_lsp, st.n1("place", 1, 0))
                        v_.tensor_tensor(eq[:, :, :] if L == 0 else hote[:, 0, :, :], over_k(iota_e), over_e(topf[b]),
                                         ALU.is_equal).then_inc(s_eq, 1)
                    if L == 1 and u < K and st.on("comb"):
                        b = st.buf("comb")
                        if u == 0:
                            dve.wait_ge(d_yg, st.n1("comb", 16 * K))
                            dve.wait_ge(d_x[b], st.nbuf("comb"))
                            wait(dve, d_x2[b], st.nbuf1("comb") - 16)
                        else:
                            dve.wait_ge(s_comb, st.n1("comb", K, u))
                        v_.scalar_tensor_tensor(x2[b][:, :], yg[:, u, :],
                                                w_all[:, bass.ds(st.pair("comb") * K + u, 1)],
                                                (x2 if u else xin)[b][:, :], ALU.mult, ALU.add).then_inc(s_comb, 1)
                    if u == 2 and st.on("place"):
                        dve.wait_ge(s_ex, st.n("place"))
                        if L == 0:
                            ch.add(v_.tensor_reduce(den[:, 0:1], ex[:, 0:K], AX.X, ALU.add), "den")
                        else:
                            ch.add(v_.tensor_tensor(exm[:, :], ex[:, :], mask[st.buf("place")][:, :], ALU.mult), "exm")
                    if u == 3 and st.on("place") and L == 1:
                        ch.join("exm")
                        ch.add(v_.tensor_reduce(den[:, 0:1], exm[:, :], AX.X, ALU.add), "den")
                    if u == 4 and st.on("place"):
                        ch.join("den")
                        ch.add(v_.reciprocal(den[:, 1:2], den[:, 0:1]), "inv")
                    if u == 5 and st.on("place"):
                        b = st.buf("place")
                        ch.join("inv")
                        if L == 0:
                            v_.tensor_scalar(w_all[:, row(st.pair("place"), K)], ex[:, 0:K], den[:, 1:2], None, ALU.mult).then_inc(s_wk, 1)
                        else:
                            v_.tensor_scalar(xr[b][:, T:T + E], exm[:, :], den[:, 1:2], None, ALU.mult)\
                              .then_inc(s_wall, 1)
                    if u == 5 and st.on("back"):
                        invert(0)
                    if u == 6 and st.on("back"):
                        normalise(0)
                        invert(1)
                    if u == 7 and st.on("back"):
                        normalise(1)
                    if u == 6 and st.on("place") and L == 0:
                        b = st.buf("place")
                        hold(dve, d_list[b], st.nbuf1("place", 16 * K) - 16 * K)
                        v_.tensor_scalar(toki[b][:, :], toki[b][:, :], float(NB * P), None, ALU.add)
                    if u < 5 and norms:
                        newton(2 * u + 1)
                    if u == 5 and norms:
                        ch.join("newton")
                        v_.scalar_tensor_tensor(rstd[:, 1, :], mv[:, :, 0], -1.0, rstd[:, 0, :], ALU.mult, ALU.mult)\
                          .then_inc(s_rstd, 1)
                    if L == 0 and u == 8 and st.on("front"):
                        rotate(0)
                    if L == 0 and u == 4 and st.on("front"):
                        rotate(1)
                    if u == 8 and st.on("smax"):
                        negate_max(0)
                    if L == 1 and u == 10 and st.on("back"):
                        b = st.buf("back")
                        dve.wait_ge(s_ntp, st.n("back"))
                        dve.wait_ge(d_xres[b], st.nbuf("back"))
                        wait(dve, d_x1[b], lastbuf(st, "back"))
                        v_.scalar_tensor_tensor(x1[b][:, :], psM[item_bank(1, "NT")][:, 0:T], bias[:, 8:9],
                                                xres[b][:, :], ALU.add, ALU.add).then_inc(s_x1, 1)
                    if u == 8 and st.on("place"):
                        b = st.buf("place")
                        hold(dve, s_hot, st.n("place"))
                        if L == 1:
                            v_.tensor_reduce(posf[b][:, :], hot[:, :, :], AX.X, ALU.add).then_inc(s_posf, 1)
                        else:
                            here = row(st.pair("place"), K)
                            v_.tensor_reduce(place_all[:, here], hot[:, :, :], AX.X, ALU.add).then_inc(s_posf, 1)
                            v_.tensor_copy(top_all[:, here], topf[b][:, :])
                            hold(dve, s_posf, st.n("place"))
                            v_.tensor_copy(posi[b][:, :], place_all[:, here]).then_inc(s_posi, 1)
                    if u == 8 and st.on("smax"):
                        split_max(0)
                    if u == 9 and st.on("place") and L == 1:
                        b = st.buf("place")
                        dve.wait_ge(s_posf, st.n("place"))
                        v_.tensor_tensor(hotr[:, :, :], over_k(iota_r), over_e(posf[b], P), ALU.is_equal)\
                          .then_inc(s_lhs, 1)
                    if L == 0 and u == 12 and st.on("back"):
                        b = st.buf("back")
                        dve.wait_ge(s_wo, st.n("back"))
                        dve.wait_ge(d_xres[b], st.nbuf("back"))
                        wait(dve, d_x1[b], lastbuf(st, "back"))
                        v_.scalar_tensor_tensor(x1[b][:, :], psM[item_bank(0, "WO")][:, 0:T], bias[:, 4:5], xres[b][:, :],
                                                ALU.add, ALU.add).then_inc(s_x1, 1)
                    if L == 1 and u == 13 and st.on("place"):
                        ps = psM[item_bank(1, "LIST")]
                        dve.wait_ge(s_lsp, st.n1("place"))
                        ch.join()
                        ch.add(v_.scalar_tensor_tensor(id_acc[:, :], ps[:, 0:E], tok0[:, 0:1], id_acc[:, :],
                                                       ALU.mult, ALU.add))
                        ch.join()
                        ch.add(v_.tensor_scalar(tok0[:, :], tok0[:, :], float(P), None, ALU.add))
                        v_.tensor_tensor(id_acc[:, :], ps[:, E:2 * E], id_acc[:, :], ALU.add).then_inc(s_list, 1)
                        dve.wait_ge(s_list, st.n1("place"))
                    if u == 13 and st.on("route"):
                        b = st.buf("route")
                        hold(dve, s_logit, st.n("route"))
                        v_.max(top[b][:, :], logit[:, :]).then_inc(s_top, 1)
                    if u == 14 and st.on("route"):
                        b = st.buf("route")
                        hold(dve, s_top, st.n("route"))
                        hold(dve, s_ex, last(st, "route"))
                        v_.max_index(topi[b][:, :], top[b][:, :], logit[:, :])
                        v_.tensor_scalar(ntop[:, :], top[b][:, 0:1], -1.0, None, ALU.mult).then_inc(s_ntop, 1)
                        ch.add(v_.match_replace(rest[:, :], top[b][:, :], logit[:, :], -3.0e38), "rest")
                        ch.join("rest")
                        v_.tensor_tensor(mask[b][:, :], rest[:, :], logit[:, :], ALU.not_equal).then_inc(s_mask, 1)
                        v_.tensor_copy(topf[b][:, :], topi[b][:, :]).then_inc(s_topf, 1)
                    if u == 15 and st.on("smax"):
                        negate_max(1)
                    if u == 14 and st.on("back"):
                        b = st.buf("back")
                        dve.wait_ge(s_x1, st.n("back"))
                        wait(dve, s_xr, last(st, "back"))
                        ch.add(v_.bn_stats(stats[:, 1, :], x1[b][:, :]), "stats1")
                    if u == 15 and st.on("comb"):
                        b = st.buf("comb")
                        if L == 0:
                            dve.wait_ge(d_x[b], st.nbuf("comb"))
                        else:
                            dve.wait_ge(s_comb, st.n1("comb", K))
                        ch.add(v_.bn_stats(stats[:, 0, :], (xin, x2)[L][b][:, :]), "stats0")
                    if u == 15 and st.on("back"):
                        ch.join("stats1")
                        v_.bn_aggr(mv[:, 1, :], stats[:, 1, :]).then_inc(s_mvr, 1)
                    if u == 15 and st.on("smax"):
                        split_max(1)
                    if u == 15 and st.on("comb"):
                        wait(dve, s_xn, last(st, "comb"))
                        ch.join("stats0")
                        v_.bn_aggr(mv[:, 0, :], stats[:, 0, :]).then_inc(s_mvx, 1)

            def run(L):
                for s in range(LOOP0):
                    before = ch.n
                    body(Step(L, s))
                ch.per = 3 * (ch.n - before)
                with dve.Fori(0, LOOPN) as it:
                    ch.it = it
                    before = ch.n
                    for c in range(NB):
                        body(Step(L, LOOP0 + c, it))
                    assert ch.n - before == ch.per
                ch.it = 0
                ch.n += ch.per * (LOOPN - 1)
                for s in range(LOOP0 + NB * LOOPN, STEPS):
                    body(Step(L, s))

            def link(ins):
                ch.add(ins)
                ch.join()

            def tiles_table():
                link(v_.tensor_tensor(cnt[:, 0, :], total[:, :], base0[:, :], ALU.subtract))
                link(v_.tensor_scalar(cnti[:, :], cnt[:, 0, :], float(P - 1), None, ALU.add))
                link(v_.tensor_scalar(cnti[:, :], cnti[:, :], 7, None, ALU.logical_shift_right))
                link(v_.tensor_copy(cnt[:, 1, :], cnti[:, :]))
                v_.tensor_scalar(cnt[:, 2, :], cnt[:, 1, :], 1.0, None, ALU.max).then_inc(s_r1, 1)
                link(v_.tensor_scalar(tri_f[:, :], iota_e[0:E, :], part1[0:E, 0:1], None, ALU.subtract))
                link(v_.tensor_scalar(tri_f[:, :], tri_f[:, :], -1.0, None, ALU.is_ge))
                dve.wait_ge(s_r2, 1)
                v_.tensor_copy(cumT[:, :], psM[0][0:E, 0:P]).then_inc(s_r1, 1)
                dve.wait_ge(s_r2, 2)
                link(v_.tensor_copy(cnt[:, 3, :], psM[1][:, 0:E]))
                link(v_.tensor_scalar(owner[:, 0, :], slotk[:, :], cnt[:, 3, E - 1:E], None, ALU.is_ge))
                link(v_.scalar_tensor_tensor(slotk[:, :], owner[:, 0, :], -float(TOKENS * K // P), slotk[:, :],
                                             ALU.mult, ALU.add))
                for c in range(3):
                    link(v_.tensor_scalar(cmp_[:, c, :], cnt[:, 3, :], slotk[:, c:c + 1], None, ALU.is_le))
                    link(v_.tensor_tensor(cmpm[:, c, :], cmp_[:, c, :], cnt[:, 3, :], ALU.mult))
                link(v_.tensor_reduce(owner[:, 0, :], cmp_[:, :, :], AX.X, ALU.add))
                link(v_.tensor_reduce(owner[:, 1, :], cmpm[:, :, :], AX.X, ALU.max))
                link(v_.tensor_tensor(owner[:, 2, :], slotk[:, :], owner[:, 1, :], ALU.subtract))
                link(v_.tensor_scalar(owner[:, 3, :], owner[:, 2, :], float(P), None, ALU.mult))
                link(v_.scalar_tensor_tensor(owner[:, 3, :], owner[:, 0, :], float(TOKENS), owner[:, 3, :],
                                             ALU.mult, ALU.add))
                link(v_.tensor_scalar(owner[:, 0, :], owner[:, 0, :], float(E - 1), None, ALU.min))
                v_.tensor_scalar(owner[:, 1, :], owner[:, 0, :], -1.0, float(E - 1), ALU.mult, ALU.add)\
                  .then_inc(s_r3, 1)
                dve.wait_ge(s_r2, 3)
                for w in range(2):
                    ins = v_.tensor_copy(tabrow[0:1, w, :], psM[w][0:1, 0:TILES0])
                ins.then_inc(s_r3, 1)
                link(v_.tensor_tensor(cnt[:, 4, :], cnt[:, 3, :], cnt[:, 2, :], ALU.subtract))
                link(v_.scalar_tensor_tensor(cnt[:, 5, :], cnt[:, 4, :], float(P), base0[:, :],
                                             ALU.mult, ALU.subtract))

            def output_rows(t, c):
                if c == 1:
                    if not isinstance(t, int) or t:
                        hold(dve, s_row, t * 1)
                    v_.tensor_tensor(fhot[:, :, :], over_k(iota_e), over_e(top_all[:, row(t, K)]), ALU.is_equal)\
                      .then_inc(s_fhot, 1)
                elif c == 3:
                    hold(dve, s_fhot, t * 2 + 1)
                    v_.tensor_tensor(fhot[:, :, :], fhot[:, :, :], over_k(cnt[:, 5, :]), ALU.mult).then_inc(s_fhot, 1)
                elif c == 5:
                    hold(dve, s_fhot, t * 2 + 2)
                    v_.tensor_reduce(rowd[:, row(t, K)], fhot[:, :, :], AX.X, ALU.add).then_inc(s_row, 1)

            def all_rows():
                dve.wait_ge(s_row, PAIRS)
                link(v_.tensor_tensor(rowd[:, :], rowd[:, :], place_all[:, :], ALU.add))
                link(v_.tensor_copy(row_all[:, :], rowd[:, :]))

            def lists():
                link(v_.tensor_scalar(cnt[:, 0, :], id_acc[:, :], 0.0, None, ALU.is_equal))
                link(v_.tensor_scalar(cnt[:, 1, :], id_acc[:, :], -1.0, None, ALU.add))
                link(v_.tensor_scalar(cnt[:, 2, 0:1], part1[:, :], float(TOKENS), None, ALU.add))
                link(v_.scalar_tensor_tensor(cnt[:, 3, :], cnt[:, 0, :], cnt[:, 2, 0:1], cnt[:, 1, :],
                                             ALU.mult, ALU.add))
                v_.tensor_copy(idx_e[:, :], cnt[:, 3, :]).then_inc(s_r2, 1)
                dve.wait_ge(s_r2, 4)

            def slot_body(st, table):
                L = st.L
                if L == 1 and st.on("idx"):
                    b = st.buf("idx")
                    hold(dve, d_xg[b], st.nbuf("idx", 1))
                    v_.tensor_copy(idx[b][:, :], idx_e[:, bass.ds(st.job("idx"), 1)]).then_inc(s_idx, 1)
                if L == 1 and st.on("X"):
                    b = st.buf("X")
                    hold(dve, s_y, st.n("X", FB))
                    hold(dve, d_xg[b], st.nbuf("X"))
                    v_.tensor_copy(wcol[b][:, :], xg[b][:, bass.ds(st.job("X") + T, 1)]).then_inc(s_wcol, 1)
                if st.on("GU"):
                    i = st.buf("GU", 2)
                    dve.wait_ge(s_sil, st.n("GU"))
                    wait(dve, s_hp, st.n("GU", 2))
                    v_.tensor_tensor(hid[i][:, :], sil[i][:, :], psE[i][:, I:2 * I], ALU.mult).then_inc(s_hid, 1)
                if st.on("H"):
                    i = st.buf("H", 2)
                    dve.wait_ge(s_hp, st.n("H"))
                    wait(dve, s_yp, st.n("H", 2))
                    v_.tensor_copy(hT[i][:, :], (psS[2], psO)[i][0:I, 0:P]).then_inc(s_hT, 1)
                if L == 1 and st.on("D"):
                    b = st.buf("D")
                    hold(dve, s_yp, st.n("D"))
                    hold(dve, d_acc[st.buf("D", 2)], (st.pair_job("D") - 3) * 16)
                    v_.tensor_copy(idx_s[b][:, :], idx_e[:, bass.ds(st.job("D"), 1)])
                    dve.wait_ge(s_wcol, st.n("D") - JOBS[0])
                    v_.tensor_scalar(y[b], psM[st.buf("D", 2)][:, 0:T], wcol[b][:, 0:1], None, ALU.mult)\
                      .then_inc(s_y, 1)

            for L in range(2):
                if L == 1:
                    clear(1)
                    barrier(dve, 4)
                run(L)
                barrier(dve, 2 + 3 * L)
                if L == 0:
                    tiles_table()
                else:
                    lists()
                slots(L, dve, slot_body, aside=None if L else output_rows)
                if L == 0:
                    all_rows()
                    link(v_.memset(total[:, :], 0.0))
                barrier(dve, 3 + 3 * L)

        @block.tensor
        def _(pe):
            m_ = nc.tensor
            barrier(pe, 1)

            def body(st):
                L = st.L

                def scores(u):
                    b, bg, tt = st.buf("smax"), u // 2, u % 2
                    if u == 0:
                        pe.wait_ge(d_stack[b], st.nbuf("smax", 16 * 14))
                    wait(pe, s_max, st.n("smax", UNITS, u - 2))
                    m_.matmul(psS[(UNITS * (st.s0 - LAG["smax"]) + u) % 3][:, :], q2[b][:, bg, tt * P:(tt + 1) * P], k2[b][:, bg, :],
                              start=True, stop=True).then_inc(s_score, 1)

                def scores_t(u):
                    b, bg, hh = st.buf("attn"), u // 2, u % 2
                    if u % 8 == 0:
                        pe.wait_ge(d_max[u // 8][b], st.nbuf("attn", 32))
                    wait(pe, s_exp, st.n("attn", UNITS, u - 1))
                    ring = u % 2
                    for i in range(2):
                        ins = m_.matmul(psE[ring][:, i * T:(i + 1) * T],
                                        k2[b][:, bg, hh * T + i * P:hh * T + (i + 1) * P], q2[b][:, bg, :],
                                        start=True, stop=True)
                    ins.then_inc(s_st, 1)

                def values(stage, q):
                    if not st.on(stage):
                        return
                    b = st.buf(stage)
                    gr = (4 * (st.s0 - LAG[stage]) + q) % 3
                    pe.wait_ge(s_exp, st.n(stage, UNITS, 4 * q + 4))
                    pe.wait_ge(s_v, st.n(stage))
                    wait(pe, s_oev, st.n(stage, 4, q))
                    for i in range(2):
                        for j in range(4):
                            ins = m_.matmul(psO[32 * j:32 * j + 32, (q % 2) * T:(q % 2 + 1) * T],
                                            v[b][:, i, 4 * q + j, :], prob[gr][:, j, i * T:(i + 1) * T],
                                            start=(i == 0), stop=(i == 1))
                    ins.then_inc(s_pv, 1)

                def product(item, stage, ready, terms, done, n=T):
                    for semaphore, value in ready:
                        pe.wait_ge(semaphore, value)
                    ps = bank(pe, st, item)
                    for i, (lhs, rhs) in enumerate(terms):
                        if rhs is None:
                            w = lhs.shape[1] if len(lhs.shape) == 2 else 32
                            ins = m_.transpose(ps[0:w, i * P:(i + 1) * P], lhs, ident[:, :])
                        else:
                            ins = m_.matmul(ps[:, i * n:(i + 1) * n], lhs, rhs, start=True, stop=True)
                    ins.then_inc(done, 1)

                for u in range(UNITS):
                    if st.on("smax"):
                        scores(u)
                    if st.on("attn"):
                        scores_t(u)
                    if u == 3:
                        values("back", 3)
                    if u in (7, 11, 15):
                        values("attn", (u - 7) // 4)
                    if u == 0 and st.on("place"):
                        b = st.buf("place")
                        product("RK", "place", [(s_mask, st.n("place"))],
                                [(tri[:, :], mask[b][:, :]), (ones[:, :], mask[b][:, :])], s_rkp, E)
                    if u == 1 and st.on("attn"):
                        product("mT1", "attn", [(s_msp[1], st.n("attn", 2))],
                                [(msp[1][:, :, :, :].rearrange("p h a r -> p (h a r)"), None)], s_mT[1])
                    if u == 3 and st.on("front"):
                        b = st.buf("front")
                        product("K", "front", [(d_ctx[b], st.nbuf("front"))],
                                [(wbd[L][n][:, :], ctx_t[b][:, :]) for n in ("ks", "k")[L]], s_kp)
                    if u == 4 and st.on("smax"):
                        b = st.buf("smax")
                        product("V", "smax", [(d_ctx[b], st.nbuf("smax"))],
                                [(ctx_t[b][:, i * P:(i + 1) * P], wbd[L]["v"][:, :]) for i in range(2)], s_vp, P)
                    if u in (5, 6) and st.on("back"):
                        h = u - 5
                        product(f"OT{h}", "back", [(s_oev, st.n("back", 4))],
                                [(osb[:, q, h * P:(h + 1) * P], None) for q in range(GROUPS)], s_ot[h])
                    if u == 7 and st.on("front"):
                        b = st.buf("front")
                        product("Q", "front", [(s_xn, st.n("front"))],
                                [(wbd[L][n][:, :], xn[b][:, :]) for n in ("qr", "q")[L]], s_qp)
                    if u == 8 and st.on("back"):
                        product("NT", "back", [(s_nrm[0], st.n("back")), (s_nrm[1], st.n("back"))],
                                [(nrm[:, h, :], None) for h in range(2)], s_ntp)
                    if u == 10 and st.on("route"):
                        b = st.buf("route")
                        product("XT", "route", [(s_xr, st.n("route"))],
                                [(xr[b][:, i * P:(i + 1) * P], None) for i in range(2)], s_xtp)
                    if u == 11 and st.on("smax"):
                        product("mT0", "smax", [(s_msp[0], st.n("smax", 2))],
                                [(msp[0][:, :, :, :].rearrange("p h a r -> p (h a r)"), None)], s_mT[0])
                    if u == 12 and st.on("back") and L == 0:
                        product("WO", "back", [(s_nt, st.n("back"))], [(wbd[0]["o"][:, :], nt[:, :])], s_wo)
                    if u == 12 and st.on("place") and L == 1:
                        pe.wait_ge(s_lhs, st.n1("place"))
                        pe.wait_ge(s_hote, st.n1("place"))
                        ps = bank(pe, st, "LIST")
                        for k in range(K):
                            ins = m_.matmul(ps[:, 0:2 * E], hotr[:, k, :], hote[:, :, k, :],
                                            start=(k == 0), stop=(k == K - 1))
                        ins.then_inc(s_lsp, 1)
                    if u == 13 and st.on("route"):
                        pe.wait_ge(s_xT, st.n("route"))
                        ps = bank(pe, st, "LG")
                        for i in range(2):
                            ins = m_.matmul(ps[:, 0:E], xT[:, i, :], wr[L][:, i, :], start=(i == 0), stop=(i == 1))
                        ins.then_inc(s_lgp, 1)

            def slot_body(st, table):
                if st.on("X"):
                    b, i = st.buf("X"), st.buf("X", 2)
                    pe.wait_ge(d_xg[b], st.nbuf("X"))
                    for c in range(2):
                        ins = m_.transpose(psS[i][:, c * P:(c + 1) * P], xg[b][:, c * P:(c + 1) * P], ident[:, :])
                    ins.then_inc(s_xp, 1)
                if st.on("GU"):
                    i = st.buf("GU", 2)
                    pe.wait_ge(s_xgT, st.n("GU"))
                    for c in range(2):
                        ins = m_.matmul(psE[i][:, 0:2 * I], xgT[i][:, c, :],
                                        weights_of(st, "GU", table, P, 2 * I * c, 2 * I),
                                        start=(c == 0), stop=(c == 1))
                    ins.then_inc(s_gup, 1)
                if st.on("H"):
                    i = st.buf("H", 2)
                    pe.wait_ge(s_hid, st.n("H"))
                    m_.transpose((psS[2], psO)[i][0:I, 0:P], hid[i][:, :], ident[:, :]).then_inc(s_hp, 1)
                if st.on("D"):
                    i = st.buf("D", 2)
                    pe.wait_ge(s_hT, st.n("D"))
                    wait(pe, s_y, st.n("D", 2))
                    m_.matmul(psM[i][:, 0:T], hT[i][:, :],
                              weights_of(st, "D", table, I, 4 * I, T),
                              start=True, stop=True).then_inc(s_yp, 1)

            def weights_of(st, stage, table, rows, first, n):
                at = E - 1 - st.job(stage) if st.L == 1 else table[st.s0 - FLAG[stage]]
                return wt[0:rows, bass.ds(at, 1), first:first + n].rearrange("p o n -> p (o n)")

            for L in range(2):
                if L == 1:
                    barrier(pe, 4)
                steps(L, pe, body)
                barrier(pe, 2 + 3 * L)
                if L == 0:
                    pe.wait_ge(s_r1, 1)
                    m_.transpose(psM[0][0:E, 0:P], cnt[:, 2, :], ident[:, :]).then_inc(s_r2, 1)
                    pe.wait_ge(s_r1, 2)
                    m_.matmul(psM[1][:, 0:E], cumT[:, :], tri_f[:, :], start=True, stop=True).then_inc(s_r2, 1)
                    pe.wait_ge(s_r3, 1)
                    for w, column in enumerate((3, 1)):
                        for c in range(3):
                            ins = m_.matmul(psM[w][0:1, c * P:(c + 1) * P], owner[:, column, c:c + 1], ident[:, :],
                                            start=True, stop=True)
                    ins.then_inc(s_r2, 1)
                    pe.wait_ge(s_r3, 2)


                def weights(group):
                    for g in range(group, E // FB if group == PEELED else group + 1):
                        pe.wait_ge(d_w[g], 32 * FB * (L + 1))

                slots(L, pe, slot_body, None if L else look_up(mybir.EngineType.PE, 1, "D", "GU"), weights)
                barrier(pe, 3 + 3 * L)


def rotary_tables():
    half = HC // 2
    inv = (np.float32(1.0) / np.float32(10000.0) ** (np.arange(0, HC, 2, dtype=np.float32) / np.float32(HC)))
    pos = np.arange(T, dtype=np.float32)[:, None] * inv.astype(np.float32)[None, :]
    c = np.cos(pos.astype(np.float64)).astype(np.float32).T
    s = np.sin(pos.astype(np.float64)).astype(np.float32).T
    cos = np.concatenate([c, c])
    sin = np.concatenate([-s, s])
    return tuple(np.ascontiguousarray(np.broadcast_to(a[None, :, None, :], (2, HC, 8, T)).reshape(P, T))
                 for a in (cos, sin))


def kernel(**inputs):
    import concourse.bacc as bacc
    from concourse.bass_utils import run_bass_kernel_spmd

    a = {n: np.asarray(z) for n, z in inputs.items()}

    def stacked(w, roll=0):
        w = np.roll(w.reshape(4, 2, HC, -1), roll, axis=2)
        return w.transpose(3, 1, 2, 0).reshape(C, C)

    def stacked_bias(b, roll=0):
        b = np.roll(b.reshape(4, 2, HC), roll, axis=2).transpose(1, 2, 0)
        return np.repeat(b[:, :, None, :], 2, axis=2).reshape(P)

    small = np.stack([stacked(a["L0_xattn_Wq"]), stacked(a["L0_xattn_Wq"], 4),
                      stacked(a["L0_xattn_Wk"]), stacked(a["L0_xattn_Wk"], 4),
                      a["L0_xattn_Wv"].T, a["L0_xattn_Wo"].T,
                      stacked(a["L1_xattn_Wq"]), stacked(a["L1_xattn_Wk"]), a["L1_xattn_Wv"].T], axis=1)
    bias = np.stack([stacked_bias(a["L0_xattn_bq"]), stacked_bias(a["L0_xattn_bq"], 4),
                     stacked_bias(a["L0_xattn_bk"]), stacked_bias(a["L0_xattn_bk"], 4),
                     np.tile(a["L0_xattn_bo"], 2),
                     stacked_bias(a["L1_xattn_bq"]), stacked_bias(a["L1_xattn_bk"]),
                     np.tile(a["L0_xattn_bv"], 2), np.tile(a["L1_xattn_bv"], 2)], axis=1)
    arrays = {
        "x": a["x"].reshape(TOKENS, T), "ctx": a["ctx_2048"].reshape(TOKENS, T),
        "small": small, "bias": bias,
        "wr0": a["L0_ffn_W_router"].reshape(2, P, E).transpose(1, 0, 2),
        "wr1": a["L1_ffn_router_weight"].reshape(2, P, E).transpose(1, 0, 2),
    }
    for L, (g, u, d) in enumerate((("L0_ffn_W_gate", "L0_ffn_W_up", "L0_ffn_W_down"),
                                   ("L1_ffn_gate_proj", "L1_ffn_up_proj", "L1_ffn_down_proj"))):
        w = np.concatenate([a[g], a[u]], axis=2).reshape(E, 2, P, 2 * I)
        arrays[f"gu{L}"] = w.transpose(2, 0, 1, 3).reshape(P, E, 4 * I)
        arrays[f"dn{L}"] = a[d].transpose(1, 0, 2)
    arrays["cos"], arrays["sin"] = rotary_tables()
    arrays = {f"in_{n}": np.ascontiguousarray(z) for n, z in arrays.items()}

    nc = bacc.Bacc("TRN2", target_bir_lowering=False, num_devices=1)
    ap = {n[3:]: nc.dram_tensor(n, z.shape, mybir.dt.from_np(z.dtype), kind="ExternalInput").ap()
          for n, z in arrays.items()}
    out = nc.dram_tensor("out", (TOKENS + P, T), F32, kind="ExternalOutput").ap()
    wts = dict(small=ap["small"], bias=ap["bias"], wr0=ap["wr0"], wr1=ap["wr1"],
               gu=(ap["gu0"], ap["gu1"]), dn=(ap["dn0"], ap["dn1"]))
    build(nc, ap["x"], ap["ctx"], (ap["cos"], ap["sin"]), wts, out)
    r = run_bass_kernel_spmd(nc, [arrays], core_ids=[0])
    return r.results[0]["out"][:TOKENS].reshape(B, C, T)
```
